# Optimizing a Trainium2 kernel written in Bass

```python
import numpy as np
import jax
import jax.numpy as jnp

def _softmax(x, axis=-1):
    return jax.nn.softmax(x, axis=axis)
def _gelu(x):
    return jax.nn.gelu(x, approximate=True)
def _silu(x):
    return jax.nn.silu(x)
def _sigmoid(x):
    return jax.nn.sigmoid(x)
def _layernorm(x, axis=-1, eps=1e-5):
    m = jnp.mean(x, axis=axis, keepdims=True)
    v = jnp.var(x, axis=axis, keepdims=True)
    return (x - m) / jnp.sqrt(v + eps)
def _scatter_add(tgt, idx, src, axis=0):
    return tgt.at[idx].add(src)
def _segment_sum(src, seg, n):
    return jax.ops.segment_sum(src, seg, n)

kernel_name = 'mk_conv_preact_d2_conv_nhwc192_c0f3f3'

def setup_inputs(seed: int = 0):
    np.random.seed(seed)
    _w = jnp.asarray
    def _rec_inputs():
        import jax
        import jax.numpy as jnp
        _gk = jax.random.key(seed)
        x = -0.0003483 + 1 * jax.random.normal(jax.random.fold_in(_gk, 1), (2, 192, 192, 192), jnp.float32)
        return x
    x = _rec_inputs()
    def _L0_conv_setup():
        import jax, jax.numpy as jnp
        import numpy as np
        B, C, H, W = (2, 192, 192, 192)
        WS = 8
        N = WS * WS
        K = 9
        HEADS = 8
        DH = C // HEADS

        def _window_nodes(x):
            xw = x.reshape(B, C, H // WS, WS, W // WS, WS)
            xw = xw.transpose(0, 2, 4, 3, 5, 1)
            return xw.reshape(-1, N, C)

        def _window_reverse(y):
            y = y.reshape(B, H // WS, W // WS, WS, WS, C)
            return y.transpose(0, 5, 1, 3, 2, 4).reshape(B, C, H, W)

        def _knn_idx(xw):
            sq = jnp.sum(xw * xw, axis=-1)
            d2 = sq[:, :, None] + sq[:, None, :] - 2.0 * jnp.einsum('wnc,wmc->wnm', xw, xw)
            d2 = d2 + jnp.eye(N, dtype=d2.dtype) * jnp.float32(1000000000.0)
            _, idx = jax.lax.top_k(-d2, K)
            return idx
        key = jax.random.key(seed)
        ks = jax.random.split(key, 9)
        s = 1.0 / np.sqrt(C)
        return {'x': jax.random.normal(ks[0], (B, C, H, W), dtype=jnp.float32), 'Wq': jax.random.normal(ks[1], (C, C), dtype=jnp.float32) * s, 'bq': jnp.zeros((C,), jnp.float32), 'Wk': jax.random.normal(ks[2], (C, C), dtype=jnp.float32) * s, 'bk': jnp.zeros((C,), jnp.float32), 'Wv': jax.random.normal(ks[3], (C, C), dtype=jnp.float32) * s, 'bv': jnp.zeros((C,), jnp.float32), 'Wskip': jax.random.normal(ks[4], (C, C), dtype=jnp.float32) * s, 'bskip': jnp.zeros((C,), jnp.float32)}
    _L0_conv_all = _L0_conv_setup()
    _L0_conv_in = {k: v for k, v in _L0_conv_all.items() if k in ('Wq', 'bq', 'Wk', 'bk', 'Wv', 'bv', 'Wskip', 'bskip', )}
    del _L0_conv_all

    def _L1_conv_setup():
        import jax, jax.numpy as jnp
        import numpy as np
        import math

        def _selective_scan(u, delta, A, Bs, Cs, D, delta_bias):
            delta = jax.nn.softplus(delta + delta_bias[None, :, :, None])
            dl = jnp.moveaxis(delta, -1, 0)
            ul = jnp.moveaxis(u, -1, 0)
            bl = jnp.moveaxis(Bs, -1, 0)
            cl = jnp.moveaxis(Cs, -1, 0)
            h0 = jnp.zeros(u.shape[:3] + (A.shape[-1],), u.dtype)

            def step(h, inp):
                d, ut, bt, ct = inp
                h = jnp.exp(d[..., None] * A) * h + (d * ut)[..., None] * bt[:, :, None, :]
                y = jnp.einsum('bkdn,bkn->bkd', h, ct)
                return (h, y)
            _, ys = jax.lax.scan(step, h0, (dl, ul, bl, cl))
            return jnp.moveaxis(ys, 0, -1) + D[None, :, :, None] * u
        key = jax.random.key(seed)
        B, H, W, C = (8, 64, 64, 192)
        Dn, N, R, K = (192, 8, 12, 4)
        ks = jax.random.split(key, 8)
        x = jax.random.normal(ks[0], (B, H, W, C), jnp.float32)
        in_proj_w = jax.random.normal(ks[1], (2 * Dn, C), jnp.float32) * C ** (-0.5)
        conv_w = jax.random.normal(ks[2], (Dn, 1, 3, 3), jnp.float32) * 0.2
        conv_b = jnp.zeros((Dn,), jnp.float32)
        x_proj_w = jax.random.normal(ks[3], (K, R + 2 * N, Dn), jnp.float32) * Dn ** (-0.5)
        dt_std = R ** (-0.5)
        dt_projs_w = jax.random.uniform(ks[4], (K, Dn, R), jnp.float32, -dt_std, dt_std)
        dt = jnp.exp(jax.random.uniform(ks[5], (K, Dn), jnp.float32) * (math.log(0.1) - math.log(0.001)) + math.log(0.001))
        dt = jnp.clip(dt, 0.0001, None)
        dt_projs_b = dt + jnp.log(-jnp.expm1(-dt))
        A_logs = jnp.broadcast_to(jnp.log(jnp.arange(1, N + 1, dtype=jnp.float32)), (K, Dn, N)).copy()
        Ds = jnp.ones((K, Dn), jnp.float32)
        ln_w = jnp.ones((Dn,), jnp.float32)
        ln_b = jnp.zeros((Dn,), jnp.float32)
        out_proj_w = jax.random.normal(ks[6], (C, Dn), jnp.float32) * Dn ** (-0.5)
        return {'x': x, 'in_proj_w': in_proj_w, 'conv_w': conv_w, 'conv_b': conv_b, 'x_proj_w': x_proj_w, 'dt_projs_w': dt_projs_w, 'dt_projs_b': dt_projs_b, 'A_logs': A_logs, 'Ds': Ds, 'ln_w': ln_w, 'ln_b': ln_b, 'out_proj_w': out_proj_w}
    _L1_conv_all = _L1_conv_setup()
    _L1_conv_in = {k: v for k, v in _L1_conv_all.items() if k in ('in_proj_w', 'conv_w', 'conv_b', 'x_proj_w', 'dt_projs_w', 'dt_projs_b', 'A_logs', 'Ds', 'ln_w', 'ln_b', 'out_proj_w', )}
    del _L1_conv_all

    return {
        "x": x,
        "L0_conv_Wq": _L0_conv_in["Wq"],
        "L0_conv_bq": _L0_conv_in["bq"],
        "L0_conv_Wk": _L0_conv_in["Wk"],
        "L0_conv_bk": _L0_conv_in["bk"],
        "L0_conv_Wv": _L0_conv_in["Wv"],
        "L0_conv_bv": _L0_conv_in["bv"],
        "L0_conv_Wskip": _L0_conv_in["Wskip"],
        "L0_conv_bskip": _L0_conv_in["bskip"],
        "L1_conv_in_proj_w": _L1_conv_in["in_proj_w"],
        "L1_conv_conv_w": _L1_conv_in["conv_w"],
        "L1_conv_conv_b": _L1_conv_in["conv_b"],
        "L1_conv_x_proj_w": _L1_conv_in["x_proj_w"],
        "L1_conv_dt_projs_w": _L1_conv_in["dt_projs_w"],
        "L1_conv_dt_projs_b": _L1_conv_in["dt_projs_b"],
        "L1_conv_A_logs": _L1_conv_in["A_logs"],
        "L1_conv_Ds": _L1_conv_in["Ds"],
        "L1_conv_ln_w": _L1_conv_in["ln_w"],
        "L1_conv_ln_b": _L1_conv_in["ln_b"],
        "L1_conv_out_proj_w": _L1_conv_in["out_proj_w"],
    }

def reference(x, L0_conv_Wq, L0_conv_bq, L0_conv_Wk, L0_conv_bk, L0_conv_Wv, L0_conv_bv, L0_conv_Wskip, L0_conv_bskip, L1_conv_in_proj_w, L1_conv_conv_w, L1_conv_conv_b, L1_conv_x_proj_w, L1_conv_dt_projs_w, L1_conv_dt_projs_b, L1_conv_A_logs, L1_conv_Ds, L1_conv_ln_w, L1_conv_ln_b, L1_conv_out_proj_w):
    import jax
    import jax.numpy as jnp
    def _L0_conv_ref(x, Wq, bq, Wk, bk, Wv, bv, Wskip, bskip):
        import jax, jax.numpy as jnp
        import numpy as np
        B, C, H, W = (2, 192, 192, 192)
        WS = 8
        N = WS * WS
        K = 9
        HEADS = 8
        DH = C // HEADS

        def _window_nodes(x):
            xw = x.reshape(B, C, H // WS, WS, W // WS, WS)
            xw = xw.transpose(0, 2, 4, 3, 5, 1)
            return xw.reshape(-1, N, C)

        def _window_reverse(y):
            y = y.reshape(B, H // WS, W // WS, WS, WS, C)
            return y.transpose(0, 5, 1, 3, 2, 4).reshape(B, C, H, W)

        def _knn_idx(xw):
            sq = jnp.sum(xw * xw, axis=-1)
            d2 = sq[:, :, None] + sq[:, None, :] - 2.0 * jnp.einsum('wnc,wmc->wnm', xw, xw)
            d2 = d2 + jnp.eye(N, dtype=d2.dtype) * jnp.float32(1000000000.0)
            _, idx = jax.lax.top_k(-d2, K)
            return idx
        xw = _window_nodes(x)
        idx = _knn_idx(xw)
        wB = xw.shape[0]
        q = (xw @ Wq + bq).reshape(wB, N, HEADS, DH)
        kk = (xw @ Wk + bk).reshape(wB, N, HEADS, DH)
        vv = (xw @ Wv + bv).reshape(wB, N, HEADS, DH)
        w_ix = jnp.arange(wB)[:, None, None]
        kn = kk[w_ix, idx]
        vn = vv[w_ix, idx]
        scores = jnp.einsum('wnhd,wnkhd->wnkh', q, kn) / jnp.sqrt(jnp.float32(DH))
        alpha = jax.nn.softmax(scores, axis=2)
        out = jnp.einsum('wnkh,wnkhd->wnhd', alpha, vn).reshape(wB, N, C)
        out = out + xw @ Wskip + bskip
        return _window_reverse(out)

    def _L1_conv_ref(x, in_proj_w, conv_w, conv_b, x_proj_w, dt_projs_w, dt_projs_b, A_logs, Ds, ln_w, ln_b, out_proj_w):
        import jax, jax.numpy as jnp
        import numpy as np
        import math

        def _selective_scan(u, delta, A, Bs, Cs, D, delta_bias):
            delta = jax.nn.softplus(delta + delta_bias[None, :, :, None])
            dl = jnp.moveaxis(delta, -1, 0)
            ul = jnp.moveaxis(u, -1, 0)
            bl = jnp.moveaxis(Bs, -1, 0)
            cl = jnp.moveaxis(Cs, -1, 0)
            h0 = jnp.zeros(u.shape[:3] + (A.shape[-1],), u.dtype)

            def step(h, inp):
                d, ut, bt, ct = inp
                h = jnp.exp(d[..., None] * A) * h + (d * ut)[..., None] * bt[:, :, None, :]
                y = jnp.einsum('bkdn,bkn->bkd', h, ct)
                return (h, y)
            _, ys = jax.lax.scan(step, h0, (dl, ul, bl, cl))
            return jnp.moveaxis(ys, 0, -1) + D[None, :, :, None] * u
        B, H, W, C = x.shape
        K, _, Dn = x_proj_w.shape
        N = A_logs.shape[-1]
        R = dt_projs_w.shape[-1]
        L = H * W
        xz = x @ in_proj_w.T
        xf, z = jnp.split(xz, 2, axis=-1)
        xc = jnp.transpose(xf, (0, 3, 1, 2))
        xc = jax.lax.conv_general_dilated(xc, conv_w, (1, 1), [(1, 1), (1, 1)], feature_group_count=Dn, dimension_numbers=('NCHW', 'OIHW', 'NCHW')) + conv_b[None, :, None, None]
        xc = jax.nn.silu(xc)
        x_hw = xc.reshape(B, Dn, L)
        x_wh = jnp.transpose(xc, (0, 1, 3, 2)).reshape(B, Dn, L)
        x2 = jnp.stack([x_hw, x_wh], axis=1)
        xs = jnp.concatenate([x2, jnp.flip(x2, axis=-1)], axis=1)
        x_dbl = jnp.einsum('bkdl,kcd->bkcl', xs, x_proj_w)
        dts, Bsx, Csx = jnp.split(x_dbl, [R, R + N], axis=2)
        dts = jnp.einsum('bkrl,kdr->bkdl', dts, dt_projs_w)
        A = -jnp.exp(A_logs)
        out_y = _selective_scan(xs, dts, A, Bsx, Csx, Ds, dt_projs_b)
        inv_y = jnp.flip(out_y[:, 2:4], axis=-1)
        wh_y = jnp.transpose(out_y[:, 1].reshape(B, Dn, W, H), (0, 1, 3, 2)).reshape(B, Dn, L)
        invwh_y = jnp.transpose(inv_y[:, 1].reshape(B, Dn, W, H), (0, 1, 3, 2)).reshape(B, Dn, L)
        y = out_y[:, 0] + inv_y[:, 0] + wh_y + invwh_y
        y = jnp.transpose(y, (0, 2, 1)).reshape(B, H, W, Dn)
        mu = y.mean(-1, keepdims=True)
        var = y.var(-1, keepdims=True)
        y = (y - mu) / jnp.sqrt(var + 1e-05) * ln_w + ln_b
        y = y * jax.nn.silu(z)
        return y @ out_proj_w.T

    def _gn(v, G=32, eps=1e-5):
        B_, H_, W_, C_ = v.shape
        g = v.reshape(B_, H_, W_, G, C_ // G)
        m = jnp.mean(g, axis=(1, 2, 4), keepdims=True)
        s = jnp.var(g, axis=(1, 2, 4), keepdims=True)
        return ((g - m) / jnp.sqrt(s + eps)).reshape(v.shape)

    def _ln_c(v, eps=1e-6):
        m = jnp.mean(v, axis=-1, keepdims=True)
        s = jnp.var(v, axis=-1, keepdims=True)
        return (v - m) / jnp.sqrt(s + eps)

    def _ln_t(v, eps=1e-5):
        m = jnp.mean(v, axis=-1, keepdims=True)
        s = jnp.var(v, axis=-1, keepdims=True)
        return (v - m) / jnp.sqrt(s + eps)

    def _to_tokens(v):
        B_, H_, W_, C_ = v.shape
        return v.reshape(B_, H_ * W_, C_)
    def _from_tokens(t, like):
        return t.reshape(like.shape)

    x = x + _L0_conv_ref(_gn(x), L0_conv_Wq, L0_conv_bq, L0_conv_Wk, L0_conv_bk, L0_conv_Wv, L0_conv_bv, L0_conv_Wskip, L0_conv_bskip)
    x = x + _L1_conv_ref(_gn(x), L1_conv_in_proj_w, L1_conv_conv_w, L1_conv_conv_b, L1_conv_x_proj_w, L1_conv_dt_projs_w, L1_conv_dt_projs_b, L1_conv_A_logs, L1_conv_Ds, L1_conv_ln_w, L1_conv_ln_b, L1_conv_out_proj_w)
    return x


_drawn_inputs = setup_inputs


def setup_inputs(seed=0):
    import zlib

    import numpy as np

    out = dict(_drawn_inputs(seed))
    spreads = {'L0_conv_bq': (0.0, 0.337),
     'L0_conv_bk': (0.0, 0.8),
     'L0_conv_bv': (0.0, 0.1),
     'L0_conv_bskip': (0.0, 0.1),
     'L1_conv_conv_b': (0.0, 0.1),
     'L1_conv_Ds': (1.0, 0.2),
     'L1_conv_ln_w': (1.0, 0.2),
     'L1_conv_ln_b': (0.0, 0.1)}
    factors = {'L1_conv_x_proj_w': 8.0,
     'L1_conv_dt_projs_w': 8.0,
     'L1_conv_dt_projs_b': 8.0,
     'L1_conv_A_logs': 8.0}
    for name, (base, spread) in spreads.items():
        noise = np.random.default_rng([zlib.crc32(name.encode()), seed]).standard_normal(out[name].shape)
        drawn = base * np.exp(spread * noise) if base else spread * noise
        out[name] = jnp.asarray(drawn.astype(out[name].dtype))
    for name, factor in factors.items():
        out[name] = (out[name] * factor).astype(out[name].dtype)
    return out
```

```python
from contextlib import ExitStack

import concourse.bass as bass
from concourse import mybir

F32 = mybir.dt.float32
BF16 = mybir.dt.bfloat16
ALU = mybir.AluOpType
ACT = mybir.ActivationFunctionType
AX = mybir.AxisListType

B = 2
S = 192
HALF = S // 2
GROUPS = 32
GW = S // GROUPS

WS = 8
NW = S // WS
TOK = WS * WS
PAIR = 2 * TOK
HEADS = 8
DH = S // HEADS
STRIPS = B * NW
PAIRS = NW // 2
QUADS = PAIRS // 4
FAR = -5e8
GUARD = -2e38
TAKEN = -3e38
OFF = -1e30
DD = 64
NJ = S // DD
NB = S // WS
BLK = WS * WS
LINE = 2 * S
SUBS = WS // 2
LN_EPS = 1e-5
K = 4
N = 8
R = 12
NBC = 2 * B * N
XR = NBC + B * R
SPLIT = 1 / 64
C0, C1, C2 = 0.9999999708, -0.49996632, 0.327558
GN_EPS = 1e-5


def stats_phase(nc, tag, x, stats, eps):
    ROWS = 64
    T = S // ROWS
    CH = B * T
    with ExitStack() as ctx:
        def sb(name, shape, dt=F32):
            return ctx.enter_context(nc.sbuf_tensor(tag + name, shape, dt))

        def sem(name):
            return ctx.enter_context(nc.semaphore(tag + name))

        xt = [sb(f"xt{i}", [HALF, ROWS, S]) for i in range(2)]
        st = sb("st", [HALF, GROUPS, 2 * CH, 6])
        mv = sb("mv", [HALF, B * GROUPS, 2])
        mean_of = sb("mean_of", [HALF, HALF])
        tot = sb("tot", [HALF, B, GROUPS, 2])
        dev = sb("dev", [HALF, B * GROUPS])
        dev2 = sb("dev2", [HALF, B * GROUPS])
        var = sb("var", [HALF, B * GROUPS])
        sd = sb("sd", [HALF, B * GROUPS])
        rs = sb("rs", [HALF, B, GROUPS])
        wide = sb("wide", [HALF, B, 2, GROUPS, GW])
        epst = sb("epst", [HALF, 1])
        ps = ctx.enter_context(nc.psum_tensor(tag + "ps", [HALF, 2, 512], F32))
        x_in = [sem(f"x_in{i}") for i in range(2)]
        chunk_done, aggr, ones_set, summed, chain, rooted, stored = map(
            sem, ("chunk_done", "aggr", "ones_set", "summed", "chain", "rooted", "stored"))
        xv = x.rearrange("(a p) b (t n) -> a b p t n", a=2, t=T)
        with nc.Block() as block:
            @block.sync
            def _(sp):
                for b in range(B):
                    with sp.Fori(0, T) as t:
                        for i in range(2):
                            src = xv[i, b, :, bass.ds(t, 1), :].rearrange("p o n -> p (o n)")
                            sp.wait_ge(ones_set, 1)
                            sp.wait_ge(chunk_done, (t + b * T) * 2 + i + 1)
                            sp.dma_start(xt[i][:, :, :].rearrange("p r w -> p (r w)"), src).then_inc(x_in[i], 16)
                sp.wait_ge(chain, 13)
                sp.dma_start(stats.rearrange("(o b) s w -> o (b s w)", o=1),
                             wide[0:1].rearrange("o b s g w -> o (b s g w)")).then_inc(stored, 16)
                sp.wait_ge(stored, 16)

            @block.vector
            def _(dve):
                dve.memset(mean_of[:, :], 1.0 / HALF)
                dve.memset(epst[:, :], eps).then_inc(ones_set, 1)
                dve.sem_inc(chunk_done, 2)
                with dve.Fori(0, CH) as c:
                    for i in range(2):
                        dve.wait_ge(x_in[i], c * 16 + 16)
                        for g in range(GROUPS):
                            b = dve.bn_stats(st[:, g, bass.ds(2 * c + i, 1), :].rearrange("p o s -> p (o s)"),
                                             xt[i][:, :, g * GW:(g + 1) * GW])
                        b.then_inc(chunk_done, 1)
                dve.wait_ge(chunk_done, 2 * CH + 2)
                for b in range(B):
                    for g in range(GROUPS):
                        a = dve.bn_aggr(mv[:, b * GROUPS + g, :],
                                        st[:, g, b * CH:(b + 1) * CH, :].rearrange("p c s -> p (c s)"))
                a.then_inc(aggr, 1)
                dve.wait_ge(summed, 1)
                dve.tensor_copy(tot[:, :, :, :].rearrange("p b g s -> p (b g s)"), ps[:, 0, 0:2 * B * GROUPS]).then_inc(chain, 1)
                dve.wait_ge(chain, 1)
                mean = tot[:, :, :, 0].rearrange("p b g -> p (b g)")
                dve.tensor_tensor(dev[:, :], mv[:, :, 0], mean, ALU.subtract).then_inc(chain, 1)
                dve.wait_ge(chain, 2)
                dve.tensor_tensor(dev2[:, :], dev[:, :], dev[:, :], ALU.mult).then_inc(chain, 1)
                dve.wait_ge(summed, 2)
                dve.tensor_tensor(var[:, :], ps[:, 1, 0:B * GROUPS], tot[:, :, :, 1].rearrange("p b g -> p (b g)"),
                                  ALU.add).then_inc(chain, 1)
                dve.wait_ge(rooted, 1)
                r = rs[:, :, :].rearrange("p b g -> p (b g)")
                dve.reciprocal(r, sd[:, :]).then_inc(chain, 1)
                dve.wait_ge(chain, 5)
                dve.tensor_tensor(dev[:, :], r, r, ALU.mult).then_inc(chain, 1)
                dve.wait_ge(chain, 6)
                dve.scalar_tensor_tensor(out=dev[:, :], in0=var[:, :], scalar=eps, in1=dev[:, :],
                                         op0=ALU.add, op1=ALU.mult).then_inc(chain, 1)
                dve.wait_ge(chain, 7)
                dve.tensor_scalar(dev[:, :], dev[:, :], -0.5, 1.5, ALU.mult, ALU.add).then_inc(chain, 1)
                dve.wait_ge(chain, 8)
                dve.tensor_tensor(r, r, dev[:, :], ALU.mult).then_inc(chain, 1)
                dve.wait_ge(chain, 9)
                for b in range(B):
                    dve.tensor_copy(wide[:, b, 0], tot[:, b, :, 0:1].broadcast_to([HALF, GROUPS, GW])).then_inc(chain, 1)
                    dve.tensor_copy(wide[:, b, 1], rs[:, b, :].rearrange("p (g o) -> p g o", o=1)
                                    .broadcast_to([HALF, GROUPS, GW])).then_inc(chain, 1)

            @block.tensor
            def _(pe):
                pe.wait_ge(aggr, 1)
                pe.matmul(ps[:, 0, 0:2 * B * GROUPS], mean_of[:, :], mv[:, :, :].rearrange("p g s -> p (g s)"),
                          start=True, stop=True).then_inc(summed, 1)
                pe.wait_ge(chain, 3)
                pe.matmul(ps[:, 1, 0:B * GROUPS], mean_of[:, :], dev2[:, :], start=True, stop=True).then_inc(summed, 1)

            @block.scalar
            def _(act):
                act.wait_ge(chain, 4)
                act.activation(sd[:, :], var[:, :], ACT.Sqrt, bias=epst[:, 0:1]).then_inc(rooted, 1)


def attention_phase(nc, x, stats, Wq, bq, Wk, bk, Wv, bv, Ws, bs, x1):
    with ExitStack() as ctx:
        def sb(name, shape, dt=F32):
            return ctx.enter_context(nc.sbuf_tensor("a_" + name, shape, dt))

        def sem(name):
            return ctx.enter_context(nc.semaphore("a_" + name))

        def bank(name):
            return ctx.enter_context(nc.psum_tensor("a_" + name, [128, 512], F32))

        K1 = HALF + 1
        xin = [sb(f"xin{i}", [HALF, 2, WS, S]) for i in range(2)]
        xw = [sb(f"xw{i}", [K1, 2, NW, TOK]) for i in range(2)]
        xsq = [sb(f"xsq{i}", [HALF, 2, NW, TOK]) for i in range(2)]
        centred = sb("centred", [HALF, 2, WS, S])
        mean = sb("mean", [HALF, B, S])
        rstd = sb("rstd", [HALF, B, S])
        wq, wk = (sb(n, [K1, 2, 2, 4, 32]) for n in ("wq", "wk"))
        wv, ws = (sb(n, [K1, 2, S]) for n in ("wv", "ws"))
        qt = [sb(f"qt{i}", [128, 2, 4 * PAIR]) for i in range(2)]
        kd = [sb(f"kd{i}", [128, 2, 8, 4, TOK]) for i in range(2)]
        vd = sb("vd", [128, 2, 4, 2 * DH + 2])
        half_neg = sb("half_neg", [HALF, TOK])
        ident = sb("ident", [128, 128])
        diag = sb("diag", [128, TOK])
        near0, near1, near2 = (sb(n, [128, TOK + 8]) for n in ("near0", "near1", "near2"))
        best = sb("best", [128, 8])
        ninth = sb("ninth", [128, 8])
        off = sb("off", [128, TOK])
        sc = sb("sc", [128, HEADS, TOK])
        top = sb("top", [128, HEADS])
        prob = sb("prob", [128, HEADS * TOK])
        probt = sb("probt", [128, 4, PAIR])
        rsum = sb("rsum", [128, 4, 2])
        res = sb("res", [128, S])
        score_b, gram_b, v_b, out_b, turn_b, fin_b = map(bank, ("score", "gram", "v", "out", "turn", "fin"))
        qk_b = [bank("qk0"), bank("qk1")]
        OW = 4 * (2 * DH + 2)
        out_o = out_b[:, 0:OW].rearrange("p (a c) -> p a c", a=4)
        out_s = out_b[:, OW:OW + S]

        w_zero, w_in, w_ones = sem("w_zero"), sem("w_in"), sem("w_ones")
        with nc.Block() as block:
            @block.gpsimd
            def _(pool):
                for i in range(2):
                    pool.memset(kd[i][:, :, :, :, :], 0.0)
                pool.memset(ident[:, :], 0.0)
                pool.memset(diag[:, :], 0.0).then_inc(w_ones, 1)
                pool.wait_ge(w_ones, 1)
                pool.affine_select(out=ident[:, :], in_=ident[:, :], compare_op=ALU.not_equal, fill=1.0,
                                   base=0, pattern=[[-1, 128]], channel_multiplier=1).then_inc(w_ones, 1)
                pool.affine_select(out=diag[:, :], in_=diag[:, :], compare_op=ALU.not_equal, fill=FAR,
                                   base=0, pattern=[[-1, TOK]], channel_multiplier=1).then_inc(w_ones, 1)
                pool.wait_ge(w_ones, 3)
                pool.affine_select(out=diag[:, :], in_=diag[:, :], compare_op=ALU.not_equal, fill=FAR,
                                   base=-TOK, pattern=[[-1, TOK]], channel_multiplier=1)

            @block.vector
            def _(dve):
                dve.memset(wq[:, :, :, :, :], 0.0)
                dve.memset(wk[:, :, :, :, :], 0.0).then_inc(w_zero, 1)
                dve.memset(near0[:, TOK:], GUARD)
                dve.memset(ninth[:, :], GUARD)
                dve.memset(half_neg[:, :], -0.5)
                for i in range(2):
                    dve.memset(xw[i][HALF:K1, :, :, :], 1.0)
                for e in range(2):
                    mine, other = slice(e * TOK, (e + 1) * TOK), slice((1 - e) * TOK, (2 - e) * TOK)
                    dve.memset(vd[other, :, :, e * DH:(e + 1) * DH], 0.0)
                    dve.memset(vd[mine, :, :, 2 * DH + e:2 * DH + e + 1], 1.0)
                    dve.memset(vd[other, :, :, 2 * DH + e:2 * DH + e + 1], 0.0)

            @block.sync
            def _(sp):
                sp.wait_ge(w_zero, 1)
                n = 0
                for w, W, b in ((wq, Wq, bq), (wk, Wk, bk)):
                    for a in range(2):
                        sp.dma_start(w[0:HALF, a].rearrange("p m i d -> p (m i) d")[:, :, 0:DH],
                                     W[a * HALF:(a + 1) * HALF, :].rearrange("p (h d) -> p h d", d=DH)).then_inc(w_in, 16)
                    sp.dma_start(w[HALF:K1, 1].rearrange("p m i d -> p (m i) d")[:, :, 0:DH],
                                 b.rearrange("(o h d) -> o h d", o=1, d=DH)).then_inc(w_in, 16)
                    n += 48
                for w, W, b in ((wv, Wv, bv), (ws, Ws, bs)):
                    sp.dma_start(w[0:HALF, :, :], W.rearrange("(a p) n -> p a n", a=2)).then_inc(w_in, 16)
                    sp.dma_start(w[HALF:K1, 1, :], b.rearrange("(o n) -> o n", o=1)).then_inc(w_in, 16)
                    n += 32
                for b in range(B):
                    for t, s in ((mean, 0), (rstd, 1)):
                        sp.dma_start(t[:, b, :], stats[b, s:s + 1, :].broadcast_to([HALF, S])).then_inc(w_in, 16)
                        n += 16
                sp.wait_ge(w_in, n)

        x_in = [sem(f"x_in{i}") for i in range(2)]
        x_out = [sem(f"x_out{i}") for i in range(2)]
        (ready, centred_done, xw_done, sq_done, qk_done, qk_taken, gram_done, picked, score_done, sc_done, exp_done,
         turned, turn_taken, v_ready, v_taken, pv_done, norm_done, fin_done, added) = map(sem, (
             "ready", "centred_done", "xw_done", "sq_done", "qk_done", "qk_taken", "gram_done", "picked", "score_done",
             "sc_done", "exp_done", "turned", "turn_taken", "v_ready", "v_taken", "pv_done", "norm_done", "fin_done",
             "added"))
        best_found, best_cut, ninth_found, ninth_cut, off_done, top_done, masked, inverted, weighed = map(sem, (
            "best_found", "best_cut", "ninth_found", "ninth_cut", "off_done", "top_done", "masked", "inverted", "weighed"))
        BODY = 2 * PAIRS
        LOOPS = STRIPS // 2
        xv = x.rearrange("(a p) s n -> p a s n", a=2)
        x1v = x1.rearrange("b (a p) (s n) -> b p a s n", a=2, s=NW)

        def strip(v, s):
            return v[:, :, bass.ds(s, 1), :].rearrange("p a o n -> p a (o n)")

        def flat(t):
            return t[:, :, :, :].rearrange("p a h w -> p a (h w)")

        with nc.Block() as block:
            @block.sync
            def _(sp):
                sp.sem_inc(ready, 1)
                for i in range(2):
                    sp.dma_start(flat(xin[i]), strip(xv, i)).then_inc(x_in[i], 16)

                def two(b, j, last):
                    it = j + b * (NW // 2)
                    for i in range(2):
                        s = 2 * it + i
                        src = None if last else strip(xv, sp.snap(s + 2))
                        dst = strip(x1v[b], 2 * j + i if last else sp.snap(2 * j + i))
                        sp.wait_ge(ready, 1)
                        sp.wait_ge(added, (s + 1) * PAIRS)
                        sp.dma_start(dst, flat(xin[i])).then_inc(x_out[i], 16)
                        if not last:
                            sp.wait_ge(ready, 1)
                            sp.wait_ge(x_out[i], it * 16 + 16)
                            sp.dma_start(flat(xin[i]), src).then_inc(x_in[i], 16)

                for b in range(B):
                    with sp.Fori(0, NW // 2 - b) as j:
                        two(b, j, False)
                two(B - 1, NW // 2 - 1, True)
                for i in range(2):
                    sp.wait_ge(x_out[i], LOOPS * 16)

            @block.gpsimd
            def _(pool):
                pool.sem_inc(pv_done, 2 * PAIRS)
                for b in range(B):
                    with pool.Fori(0, NW // 2) as j:
                        for i in range(2):
                            s = (j + b * (NW // 2)) * 2 + i
                            pool.wait_ge(x_in[i], (j + b * (NW // 2)) * 16 + 16)
                            pool.wait_ge(xw_done, s)
                            pool.tensor_tensor(centred[:, :, :, :].rearrange("p a h w -> p (a h) w"),
                                               xin[i][:, :, :, :].rearrange("p a h w -> p (a h) w"),
                                               mean[:, b:b + 1, :].broadcast_to([HALF, 2 * WS, S]),
                                               ALU.subtract).then_inc(centred_done, 1)
                            pool.wait_ge(centred_done, s + 1)
                            pool.wait_ge(pv_done, (s + 1) * PAIRS)
                            for a in range(2):
                                m = pool.tensor_tensor(
                                    xw[i][0:HALF, a].rearrange("p n (h w) -> p n h w", w=WS),
                                    centred[:, a].rearrange("p h (n w) -> p n h w", w=WS),
                                    rstd[:, b, :].rearrange("p (n o w) -> p n o w", o=1, w=WS)
                                    .broadcast_to([HALF, NW, WS, WS]), ALU.mult)
                            m.then_inc(xw_done, 1)
                            pool.wait_ge(xw_done, s + 1)
                            pool.tensor_tensor(xsq[i][:, :, :, :], xw[i][0:HALF], xw[i][0:HALF], ALU.mult).then_inc(sq_done, 1)

            def flow(eng, body):
                with eng.Fori(0, LOOPS - 1) as it:
                    body(it, False)
                body(LOOPS - 1, True)

            def nxt(it, p, by=1):
                return (it, p + by) if p + by < BODY else (it + 1, p + by - BODY)

            @block.tensor
            def _(pe):
                def queries_keys(it, p):
                    i, quad = p // PAIRS, p // 4
                    Q = it * (BODY // 4) + quad
                    first = isinstance(it, int) and it == 0 and p == 0
                    if p % PAIRS == 0:
                        pe.wait_ge(sq_done, it * 2 + i + 1)
                    for c, (w, m) in enumerate(((wq, 0), (wq, 1), (wk, 0), (wk, 1))):
                        if not (first and c < 2):
                            pe.wait_ge(qk_taken, Q * 4 + c - 1)
                        for a, rows in ((0, HALF), (1, K1)):
                            mm = pe.matmul(qk_b[c % 2][:, :], w[0:rows, a, m].rearrange("p i d -> p (i d)"),
                                           xw[i][0:rows, a, (quad % QUADS) * 8:(quad % QUADS) * 8 + 8, :]
                                           .rearrange("p n t -> p (n t)"), start=a == 0, stop=a == 1)
                        mm.then_inc(qk_done, 1)

                def gram(it, p):
                    i, g = p // PAIRS, it * BODY + p
                    if not (isinstance(g, int) and g == 0):
                        pe.wait_ge(picked, g)
                    for w in range(2):
                        n = 2 * (p % PAIRS) + w
                        o = gram_b[w * TOK:(w + 1) * TOK, 0:TOK]
                        for a in range(2):
                            pe.matmul(o, xw[i][0:HALF, a, n, :], xw[i][0:HALF, a, n, :], start=a == 0, stop=False)
                        for a in range(2):
                            mm = pe.matmul(o, half_neg[:, :], xsq[i][:, a, n, :], start=False, stop=a == 1)
                    mm.then_inc(gram_done, 1)

                def scores(it, p):
                    g = it * BODY + p
                    if p % 4 == 0:
                        pe.wait_ge(qk_taken, (it * (BODY // 4) + p // 4 + 1) * 4)
                    if not (isinstance(g, int) and g == 0):
                        pe.wait_ge(masked, g)
                    for w in range(2):
                        n = 2 * (p % 4) + w
                        for m in range(2):
                            mm = pe.matmul(score_b[w * TOK:(w + 1) * TOK, m * 256:(m + 1) * 256],
                                           qt[p // 4 % 2][:, m, n * TOK:(n + 1) * TOK],
                                           kd[p // 4 % 2][:, m, n].rearrange("p i t -> p (i t)"), start=True, stop=True)
                    mm.then_inc(score_done, 1)

                def values(it, p):
                    i, g = p // PAIRS, it * BODY + p
                    if not (isinstance(g, int) and g == 0):
                        pe.wait_ge(v_taken, g)
                    for w in range(2):
                        n = 2 * (p % PAIRS) + w
                        for e in range(2):
                            for a, rows in ((0, HALF), (1, K1)):
                                mm = pe.matmul(v_b[e * TOK:(e + 1) * TOK, w * HALF:(w + 1) * HALF], xw[i][0:rows, a, n, :],
                                               wv[0:rows, a, :].rearrange("p (h e d) -> p e h d", e=2, d=DH)[:, e],
                                               start=a == 0, stop=a == 1)
                    mm.then_inc(v_ready, 1)

                def turn(it, p):
                    pe.wait_ge(exp_done, it * BODY + p + 1)
                    for a in range(4):
                        mm = pe.transpose(turn_b[:, a * 128:(a + 1) * 128], prob[:, a * 128:(a + 1) * 128], ident[:, :])
                    mm.then_inc(turned, 1)

                def weigh(it, p):
                    i, g = p // PAIRS, it * BODY + p
                    pe.wait_ge(turn_taken, g + 1)
                    pe.wait_ge(v_taken, g + 1)
                    if not (isinstance(g, int) and g == 0):
                        pe.wait_ge(norm_done, g)
                    for w in range(2):
                        for a in range(4):
                            pe.matmul(out_o[w * TOK:(w + 1) * TOK, a, :], probt[:, a, w * TOK:(w + 1) * TOK],
                                      vd[:, w, a, :], start=True, stop=True)
                    n = 2 * (p % PAIRS)
                    for a, rows in ((0, HALF), (1, K1)):
                        mm = pe.matmul(out_s, xw[i][0:rows, a, n:n + 2, :].rearrange("p n t -> p (n t)"),
                                       ws[0:rows, a, :], start=a == 0, stop=a == 1)
                    mm.then_inc(pv_done, 1)

                def back(it, p):
                    g = it * BODY + p
                    pe.wait_ge(norm_done, g + 1)
                    if not (isinstance(g, int) and g == 0):
                        pe.wait_ge(added, g)
                    for a in range(2):
                        mm = pe.transpose(fin_b[0:HALF, a * 128:(a + 1) * 128], res[:, a * HALF:(a + 1) * HALF], ident[:, :])
                    mm.then_inc(fin_done, 1)

                pe.wait_ge(ready, 1)
                queries_keys(0, 0)
                gram(0, 0)
                scores(0, 0)
                values(0, 0)

                def body(it, last):
                    for p in range(BODY):
                        more = not (last and p == BODY - 1)
                        turn(it, p)
                        if more:
                            gram(*nxt(it, p))
                            scores(*nxt(it, p))
                        weigh(it, p)
                        if more:
                            values(*nxt(it, p))
                        back(it, p)
                        if p % 4 == 2 and not (last and p + 2 >= BODY):
                            queries_keys(*nxt(it, p, 2))

                flow(pe, body)

            @block.scalar
            def _(act):
                def take_qk(it, p):
                    quad = p // 4
                    Q = it * (BODY // 4) + quad
                    for m in range(2):
                        act.wait_ge(qk_done, Q * 4 + m + 1)
                        act.activation(qt[quad % 2][:, m, :], qk_b[m][:, :], ACT.Copy).then_inc(qk_taken, 1)
                    for m in range(2):
                        act.wait_ge(qk_done, Q * 4 + m + 3)
                        for h in range(4):
                            rows = slice(32 * h, 32 * h + 32)
                            e = act.activation(kd[quad % 2][rows, m, :, h, :],
                                               qk_b[m][rows, :].rearrange("p (n t) -> p n t", t=TOK), ACT.Copy)
                        e.then_inc(qk_taken, 1)

                def exps(it, p):
                    g = it * BODY + p
                    act.wait_ge(sc_done, g + 1)
                    act.activation(prob[:, :], sc[:, :, :].rearrange("p h t -> p (h t)"), ACT.Exp,
                                   scale=float(DH) ** -0.5).then_inc(exp_done, 1)

                act.wait_ge(ready, 1)
                take_qk(0, 0)
                exps(0, 0)

                def body(it, last):
                    for p in range(BODY):
                        g = it * BODY + p
                        act.wait_ge(turned, g + 1)
                        act.wait_ge(pv_done, g + 2 * PAIRS)
                        act.activation(probt[:, :, :].rearrange("p a t -> p (a t)"), turn_b[:, :], ACT.Copy).then_inc(turn_taken, 1)
                        if not (last and p == BODY - 1):
                            exps(*nxt(it, p))
                        if p % 4 == 2 and not (last and p + 2 >= BODY):
                            take_qk(*nxt(it, p, 2))

                flow(act, body)

            @block.vector
            def _(dve):
                def alone(s, value):
                    dve.wait_ge(ready, 1)
                    dve.wait_ge(s, value)

                def pick(it, p):
                    g = it * BODY + p
                    dve.wait_ge(gram_done, g + 1)
                    dve.tensor_tensor(near0[:, 0:TOK], gram_b[:, 0:TOK], diag[:, :], ALU.add).then_inc(picked, 1)
                    alone(picked, g + 1)
                    dve.max(best[:, :], near0[:, 0:TOK]).then_inc(best_found, 1)
                    alone(best_found, g + 1)
                    dve.match_replace(near1[:, :], best[:, :], near0[:, :], TAKEN).then_inc(best_cut, 1)
                    dve.wait_ge(best_cut, g + 1)
                    dve.tensor_reduce(ninth[:, 0:1], near1[:, 0:TOK], AX.X, ALU.max).then_inc(ninth_found, 1)
                    alone(ninth_found, g + 1)
                    dve.match_replace(near2[:, :], ninth[:, :], near1[:, :], TAKEN).then_inc(ninth_cut, 1)
                    dve.wait_ge(ninth_cut, g + 1)
                    dve.tensor_scalar(off[:, :], near2[:, 0:TOK], 0.5 * (GUARD + TAKEN), OFF, ALU.is_gt, ALU.mult).then_inc(off_done, 1)

                def soften(it, p):
                    g = it * BODY + p
                    dve.wait_ge(score_done, g + 1)
                    dve.wait_ge(off_done, g + 1)
                    if not (isinstance(g, int) and g == 0):
                        dve.wait_ge(exp_done, g)
                    dve.tensor_tensor(sc[:, :, :], score_b[:, :].rearrange("p (h t) -> p h t", t=TOK),
                                      off[:, :].rearrange("p (o t) -> p o t", o=1).broadcast_to([128, HEADS, TOK]),
                                      ALU.add).then_inc(masked, 1)
                    dve.wait_ge(masked, g + 1)
                    dve.tensor_reduce(top[:, :], sc[:, :, :], AX.X, ALU.max).then_inc(top_done, 1)
                    dve.wait_ge(top_done, g + 1)
                    dve.tensor_tensor(sc[:, :, :], sc[:, :, :],
                                      top[:, :].rearrange("p (h o) -> p h o", o=1).broadcast_to([128, HEADS, TOK]),
                                      ALU.subtract).then_inc(sc_done, 1)

                def take_v(it, p):
                    g = it * BODY + p
                    dve.wait_ge(v_ready, g + 1)
                    for e in range(2):
                        rows = slice(e * TOK, (e + 1) * TOK)
                        t = dve.tensor_copy(vd[rows, :, :, e * DH:(e + 1) * DH].rearrange("p w a d -> p (w a) d"),
                                            v_b[rows, 0:S].rearrange("p (n d) -> p n d", d=DH))
                    t.then_inc(v_taken, 1)

                def normalise(it, p):
                    g = it * BODY + p
                    dve.wait_ge(pv_done, g + 1 + 2 * PAIRS)
                    dve.reciprocal(rsum[:, :, :], out_o[:, :, 2 * DH:]).then_inc(inverted, 1)
                    dve.wait_ge(inverted, g + 1)
                    dve.tensor_tensor(res[:, :].rearrange("p (a e d) -> p a e d", a=4, e=2),
                                      out_o[:, :, 0:2 * DH].rearrange("p a (e d) -> p a e d", e=2),
                                      rsum[:, :, :].rearrange("p a (e o) -> p a e o", o=1).broadcast_to([128, 4, 2, DH]),
                                      ALU.mult).then_inc(weighed, 1)
                    dve.wait_ge(weighed, g + 1)
                    dve.tensor_tensor(res[:, :], out_s, res[:, :], ALU.add).then_inc(norm_done, 1)

                def add_up(it, p):
                    i, g = p // PAIRS, it * BODY + p
                    dve.wait_ge(fin_done, g + 1)
                    c = 2 * WS * (p % PAIRS)
                    for a in range(2):
                        v = xin[i][:, a, :, c:c + 2 * WS].rearrange("p h (n w) -> p n h w", w=WS)
                        r = dve.tensor_tensor(v, fin_b[0:HALF, a * 128:(a + 1) * 128]
                                              .rearrange("p (n h w) -> p n h w", n=2, w=WS), v, ALU.add)
                    r.then_inc(added, 1)

                dve.wait_ge(ready, 1)
                pick(0, 0)
                soften(0, 0)
                take_v(0, 0)

                def body(it, last):
                    for p in range(BODY):
                        more = not (last and p == BODY - 1)
                        if more:
                            pick(*nxt(it, p))
                            soften(*nxt(it, p))
                        normalise(it, p)
                        if more:
                            take_v(*nxt(it, p))
                        add_up(it, p)

                flow(dve, body)


def project_phase(nc, x1, stats, w_in_t, xf, z):
    CH = 4
    with ExitStack() as ctx:
        def sb(name, shape, dt=F32):
            return ctx.enter_context(nc.sbuf_tensor("p_" + name, shape, dt))

        def sem(name):
            return ctx.enter_context(nc.semaphore("p_" + name))

        def bank(name):
            return ctx.enter_context(nc.psum_tensor("p_" + name, [128, 512], F32))

        xt = [sb(f"xt{i}", [HALF, 2 * CH, S]) for i in range(2)]
        xn = [sb(f"xn{i}", [HALF, 2, LINE]) for i in range(2)]
        xo = [sb(f"xo{i}", [128, NJ, CH * S]) for i in range(2)]
        w = sb("w", [HALF, 2, 2 * S])
        gn = sb("gn", [HALF, B, 2, 2])
        ident = sb("ident", [128, 128])
        zero = sb("zero", [128, S])
        turn_b = [bank("turn0"), bank("turn1")]
        out_b = [bank(f"out{m}") for m in range(2 * NJ)]
        w_zero, w_in, w_pad, w_set = sem("w_zero"), sem("w_in"), sem("w_pad"), sem("w_set")
        x_in = [sem(f"x_in{i}") for i in range(2)]
        o_out = [sem(f"o_out{i}") for i in range(2)]
        turned, normed, multiplied, taken_v, taken_a = map(sem, ("turned", "normed", "multiplied", "taken_v", "taken_a"))
        UNITS = S // CH
        xv = x1.rearrange("b (t l) (f p c) -> b p t (l f) c", l=CH, f=2, c=S)
        STEPS = B * UNITS * 2

        with nc.Block() as block:
            @block.gpsimd
            def _(pool):
                pool.memset(ident[:, :], 0.0).then_inc(w_set, 1)
                pool.wait_ge(w_set, 1)
                pool.affine_select(out=ident[:, :], in_=ident[:, :], compare_op=ALU.not_equal, fill=1.0,
                                   base=0, pattern=[[-1, 128]], channel_multiplier=1)
                pool.memset(zero[:, :], 0.0).then_inc(w_zero, 1)

            @block.sync
            def _(sp):
                sp.dma_start(w[:, :, :], w_in_t.rearrange("(a p) n -> p a n", a=2)).then_inc(w_in, 16)
                n = 16
                with nc.allow_non_contiguous_dma("one column of the statistics"):
                    for b in range(B):
                        for s in range(2):
                            sp.dma_start(gn[:, b, s, :], stats[b, s, :].rearrange("(a p) -> p a", a=2)).then_inc(w_in, 16)
                            n += 16
                sp.wait_ge(w_zero, 1)
                for lo, hi in ((0, 128), (128, S)):
                    for row in (0, S + 1):
                        for b in range(B):
                            sp.dma_start(xf[lo:hi, b, row, :], zero[0:hi - lo, :]).then_inc(w_pad, 16)
                sp.wait_ge(w_in, n)
                sp.wait_ge(w_pad, 16 * 4 * B)

        with nc.Block() as block:
            @block.sync
            def _(sp):
                for b in range(B):
                    with sp.Fori(0, UNITS // 2) as t:
                        for i in range(2):
                            src = xv[b, :, bass.ds(sp.snap(2 * t + i), 1), :, :].rearrange("p o k c -> p (o k) c")
                            u = (t + b * (UNITS // 2)) * 2 + i
                            sp.wait_ge(w_in, 16)
                            sp.wait_ge(turned, u * 2 + 2)
                            sp.dma_start(xt[i][:, :, :], src).then_inc(x_in[i], 16)

            @block.gpsimd
            def _(pool):
                for b in range(B):
                    with pool.Fori(0, UNITS // 2) as t:
                        for i in range(2):
                            u = (t + b * (UNITS // 2)) * 2 + i
                            first = t * (2 * CH) + i * CH
                            pool.wait_ge(taken_a, u * 2 + 3)
                            pool.wait_ge(taken_v, u * 2 + 3)
                            rows = xf[:, b, bass.ds(first + 1, CH), :].rearrange("d r w -> d (r w)")
                            zs = z[:, b, bass.ds(first * S, CH * S)]
                            for dst, src in ((rows[0:128], xo[i][:, 0, :]), (rows[128:S], xo[i][0:DD, 1, :]),
                                             (zs[0:DD], xo[i][DD:128, 1, :]), (zs[DD:S], xo[i][:, 2, :])):
                                pool.dma_start(dst, src).then_inc(o_out[i], 16)
                for i in range(2):
                    pool.wait_ge(o_out[i], B * (UNITS // 2) * 64)

            def flow(eng, body):
                for b in range(B):
                    with eng.Fori(0, UNITS // 2 - 1) as t:
                        body(b, t, (b, t + 1))
                    body(b, UNITS // 2 - 1, (b + 1, 0) if b < B - 1 else None)

            def step(b, t, e):
                return (t + b * (UNITS // 2)) * 4 + e

            @block.tensor
            def _(pe):
                pe.sem_inc(turned, 4)
                pe.sem_inc(multiplied, 1)

                def turn(b, t, e):
                    s = step(b, t, e)
                    if e % 2 == 0:
                        pe.wait_ge(x_in[e // 2], (t + b * (UNITS // 2)) * 16 + 16)
                    if not (isinstance(s, int) and s == 0):
                        pe.wait_ge(normed, s)
                    for a in range(2):
                        for k in range(4):
                            mm = pe.transpose(turn_b[a][0:HALF, k * HALF:(k + 1) * HALF],
                                              xt[e // 2][:, (e % 2) * 4 + k, a * HALF:(a + 1) * HALF], ident[0:HALF, 0:HALF])
                    mm.then_inc(turned, 1)

                def multiply(b, t, e):
                    s = step(b, t, e)
                    pe.wait_ge(normed, s + 1)
                    pe.wait_ge(taken_a, s)
                    pe.wait_ge(taken_v, s)
                    for m in range(NJ):
                        for a in range(2):
                            mm = pe.matmul(out_b[(e % 2) * NJ + m][:, 0:LINE], w[:, a, m * 128:(m + 1) * 128],
                                           xn[e % 2][:, a, :], start=a == 0, stop=a == 1)
                    mm.then_inc(multiplied, 1)

                turn(0, 0, 0)

                def body(b, t, after):
                    for e in range(4):
                        if e < 3:
                            turn(b, t, e + 1)
                        elif after:
                            turn(*after, 0)
                        multiply(b, t, e)

                flow(pe, body)

            @block.vector
            def _(dve):
                dve.sem_inc(taken_v, 1)

                def norm(b, t, e):
                    s = step(b, t, e)
                    dve.wait_ge(turned, s + 5)
                    dve.wait_ge(multiplied, s)
                    for a in range(2):
                        m = dve.tensor_scalar(xn[e % 2][:, a, :], turn_b[a][0:HALF, 0:LINE], gn[:, b, 0, a:a + 1],
                                              gn[:, b, 1, a:a + 1], ALU.subtract, ALU.mult)
                    m.then_inc(normed, 1)

                norm(0, 0, 0)

                def body(b, t, after):
                    for e in range(4):
                        if e < 3:
                            norm(b, t, e + 1)
                        elif after:
                            norm(*after, 0)
                        s = step(b, t, e)
                        dve.wait_ge(multiplied, s + 2)
                        if e % 2 == 0:
                            dve.wait_ge(o_out[e // 2], (t + b * (UNITS // 2)) * 64)
                        cols = slice((e % 2) * LINE, (e % 2 + 1) * LINE)
                        dve.tensor_copy(xo[e // 2][:, 0, cols], out_b[(e % 2) * NJ][:, 0:LINE])
                        dve.tensor_copy(xo[e // 2][0:DD, 1, cols], out_b[(e % 2) * NJ + 1][0:DD, 0:LINE]).then_inc(taken_v, 1)

                flow(dve, body)

            @block.scalar
            def _(act):
                act.sem_inc(taken_a, 1)

                def body(b, t, after):
                    for e in range(4):
                        s = step(b, t, e)
                        act.wait_ge(multiplied, s + 2)
                        if e % 2 == 0:
                            act.wait_ge(o_out[e // 2], (t + b * (UNITS // 2)) * 64)
                        cols = slice((e % 2) * LINE, (e % 2 + 1) * LINE)
                        act.activation(xo[e // 2][DD:128, 1, cols], out_b[(e % 2) * NJ + 1][DD:128, 0:LINE], ACT.Silu)
                        act.activation(xo[e // 2][:, 2, cols], out_b[(e % 2) * NJ + 2][:, 0:LINE], ACT.Silu).then_inc(taken_a, 1)

                flow(act, body)


def conv_phase(nc, xf, conv_w, conv_b, xc):
    TAPS = 9
    PEJ = 1
    with ExitStack() as ctx:
        def sb(name, shape, dt=F32):
            return ctx.enter_context(nc.sbuf_tensor("c_" + name, shape, dt))

        def sem(name):
            return ctx.enter_context(nc.semaphore("c_" + name))

        rows_t = [[sb(f"rows{i}_{j}", [128, WS + 2, S + 2]) for j in range(NJ)] for i in range(2)]
        acc = [[sb(f"acc{i}_{j}", [128, WS, S]) for j in range(PEJ, NJ)] for i in range(2)]
        xo = [sb(f"xo{i}", [128, NJ, NB, BLK]) for i in range(2)]
        wt = sb("wt", [128, NJ, TAPS])
        bt = sb("bt", [128, NJ])
        ident = sb("ident", [128, 128])
        tap = sb("tap", [128, TAPS, 128])
        banks = [ctx.enter_context(nc.psum_tensor(f"c_b{q}", [128, 512], F32)) for q in range(SUBS)]
        w_in, w_set, w_edge = sem("w_in"), sem("w_set"), sem("w_edge")
        r_in = [[sem(f"r_in{i}_{j}") for j in range(NJ)] for i in range(2)]
        o_out = [sem(f"o_out{i}") for i in range(2)]
        ready, pe_done, acc_link, acc_done, act_done = map(sem, ("ready", "pe_done", "acc_link", "acc_done", "act_done"))
        with nc.Block() as block:
            @block.gpsimd
            def _(pool):
                pool.memset(ident[:, :], 0.0).then_inc(w_set, 1)
                pool.wait_ge(w_set, 1)
                pool.affine_select(out=ident[:, :], in_=ident[:, :], compare_op=ALU.not_equal, fill=1.0,
                                   base=0, pattern=[[-1, 128]], channel_multiplier=1).then_inc(w_set, 1)

            @block.sync
            def _(sp):
                n = 0
                with nc.allow_non_contiguous_dma("weights, once"):
                    for b in range(B):
                        rows = slice(b * DD, (b + 1) * DD)
                        sp.dma_start(wt[rows, :, :], conv_w.rearrange("(j p) t -> p j t", p=DD)).then_inc(w_in, 16)
                        sp.dma_start(bt[rows, :], conv_b.rearrange("(j p) -> p j", p=DD)).then_inc(w_in, 16)
                        n += 32
                sp.wait_ge(w_in, n)

            @block.vector
            def _(dve):
                for i in range(2):
                    for j in range(NJ):
                        for c in (0, S + 1):
                            dve.memset(rows_t[i][j][:, :, c:c + 1], 0.0)
                dve.wait_ge(w_in, 64)
                dve.wait_ge(w_set, 2)
                for t in range(TAPS):
                    dve.tensor_scalar(tap[:, t, :], ident[:, :], wt[:, 0, t:t + 1], None, ALU.mult)

        with nc.Block() as block:
            @block.sync
            def _(sp):
                with sp.Fori(0, NB // 2) as t:
                    for i in range(2):
                        c = sp.snap(2 * t + i)
                        srcs = [[xf[j * DD:(j + 1) * DD, b, bass.ds(sp.snap(c * WS), WS + 2), :] for b in range(B)]
                                for j in range(NJ)]
                        sp.wait_ge(ready, 1)
                        sp.wait_ge(act_done, c)
                        for j in range(NJ):
                            for b in range(B):
                                sp.dma_start(rows_t[i][j][b * DD:(b + 1) * DD, :, 1:S + 1], srcs[j][b]).then_inc(r_in[i][j], 16)

            @block.gpsimd
            def _(pool):
                pool.sem_inc(ready, 1)
                with pool.Fori(0, NB // 2) as t:
                    for i in range(2):
                        pool.wait_ge(act_done, 2 * t + i + 2)
                        pool.dma_start(xc[:, :, bass.ds(2 * t + i, 1), :, :].rearrange("p j o b n -> p j (o b n)"),
                                       xo[i][:, :, :, :].rearrange("p j b n -> p j (b n)")).then_inc(o_out[i], 16)
                for i in range(2):
                    pool.wait_ge(o_out[i], (NB // 2) * 16)

            @block.tensor
            def _(pe):
                pe.wait_ge(ready, 1)
                with pe.Fori(0, NB // 2) as t:
                    for i in range(2):
                        c = 2 * t + i
                        pe.wait_ge(r_in[i][0], t * 32 + 32)
                        pe.wait_ge(act_done, c + 1)
                        for q in range(SUBS):
                            for k in range(TAPS):
                                mm = pe.matmul(banks[q][:, 0:LINE], tap[:, k, :],
                                               rows_t[i][0][:, 2 * q + k // 3:2 * q + k // 3 + 2, k % 3:k % 3 + S],
                                               start=k == 0, stop=k == TAPS - 1)
                            mm.then_inc(pe_done, 1)

            @block.vector
            def _(dve):
                dve.wait_ge(ready, 1)
                with dve.Fori(0, NB // 2) as t:
                    for i in range(2):
                        c = 2 * t + i
                        dve.wait_ge(act_done, c)
                        for k in range(TAPS):
                            for j in range(PEJ, NJ):
                                if k == 0:
                                    dve.wait_ge(r_in[i][j], t * 32 + 32)
                                a = acc[i][j - PEJ][:, :, :]
                                v = rows_t[i][j][:, k // 3:k // 3 + WS, k % 3:k % 3 + S]
                                if k == 0:
                                    m = dve.tensor_scalar(a, v, wt[:, j, 0:1], None, ALU.mult)
                                else:
                                    dve.wait_ge(acc_link, (c * TAPS + k - 1) * (NJ - PEJ) + j - PEJ + 1)
                                    m = dve.scalar_tensor_tensor(out=a, in0=v, scalar=wt[:, j, k:k + 1], in1=a,
                                                                 op0=ALU.mult, op1=ALU.add)
                                m.then_inc(acc_link, 1)

            @block.scalar
            def _(act):
                act.wait_ge(ready, 1)
                act.sem_inc(act_done, 1)

                def out(i, j):
                    return xo[i][:, j].rearrange("p b (h w) -> p h b w", w=WS)

                with act.Fori(0, NB // 2) as t:
                    for i in range(2):
                        c = 2 * t + i
                        act.wait_ge(o_out[i], t * 16)
                        for q in range(SUBS):
                            act.wait_ge(pe_done, c * SUBS + q + 1)
                            act.activation(out(i, 0)[:, 2 * q:2 * q + 2], banks[q][:, 0:LINE]
                                           .rearrange("p (h b w) -> p h b w", h=2, w=WS), ACT.Silu, bias=bt[:, 0:1])
                        for j in range(PEJ, NJ):
                            act.wait_ge(acc_link, ((c + 1) * TAPS - 1) * (NJ - PEJ) + j - PEJ + 1)
                            m = act.activation(out(i, j), acc[i][j - PEJ][:, :, :].rearrange("p h (b w) -> p h b w", w=WS),
                                               ACT.Silu, bias=bt[:, j:j + 1])
                        m.then_inc(act_done, 1)


def final_phase(nc, ysum, z, x1, ln_w, ln_b, w_out_t, out):
    with ExitStack() as ctx:
        def sb(name, shape, dt=F32):
            return ctx.enter_context(nc.sbuf_tensor("f_" + name, shape, dt))

        def sem(name):
            return ctx.enter_context(nc.semaphore("f_" + name))

        def bank(name):
            return ctx.enter_context(nc.psum_tensor("f_" + name, [128, 512], F32))

        TT = WS * S // 128
        T3 = LINE // 128
        yt = [sb(f"yt{i}", [128, NJ, NB, BLK]) for i in range(2)]
        zt = [sb(f"zt{i}", [128, NJ, WS * S]) for i in range(2)]
        rt = [sb(f"rt{i}", [128, B, TT, S]) for i in range(2)]
        yc = [sb(f"yc{i}", [128, NJ, LINE]) for i in range(2)]
        sq = [sb(f"sq{i}", [128, NJ, LINE]) for i in range(2)]
        sd = [sb(f"sd{i}", [128, LINE]) for i in range(2)]
        gated = [sb(f"gated{i}", [128, NJ, LINE]) for i in range(2)]
        mean_of = sb("mean_of", [128, 128])
        wo = sb("wo", [128, NJ, S])
        lnw = sb("lnw", [128, NJ])
        lnb = sb("lnb", [128, NJ])
        epst = sb("epst", [128, 1])
        mean_b, var_b = bank("mean"), bank("var")
        out_b = [[bank(f"out{t}_{b}") for b in range(B)] for t in range(T3)]
        w_in = sem("w_in")
        with nc.Block() as block:
            @block.sync
            def _(sp):
                n = 0
                with nc.allow_non_contiguous_dma("weights, once"):
                    for b in range(B):
                        rows = slice(b * DD, (b + 1) * DD)
                        sp.dma_start(wo[rows, :, :], w_out_t.rearrange("(j p) c -> p j c", p=DD)).then_inc(w_in, 16)
                        sp.dma_start(lnw[rows, :], ln_w.rearrange("(j p) -> p j", p=DD)).then_inc(w_in, 16)
                        sp.dma_start(lnb[rows, :], ln_b.rearrange("(j p) -> p j", p=DD)).then_inc(w_in, 16)
                        n += 48
                sp.wait_ge(w_in, n)

            @block.vector
            def _(dve):
                dve.memset(epst[:, :], LN_EPS)
                for b in range(B):
                    for c in range(B):
                        dve.memset(mean_of[b * DD:(b + 1) * DD, c * DD:(c + 1) * DD], 1.0 / S if b == c else 0.0)

        c_in = [sem(f"c_in{i}") for i in range(2)]
        r_out = [sem(f"r_out{i}") for i in range(2)]
        ready, mean_done, yc_done, sq_done, var_done, sd_done, inv_done, scaled, shifted, gated_done, out_done, added = map(
            sem, ("ready", "mean_done", "yc_done", "sq_done", "var_done", "sd_done", "inv_done", "scaled", "shifted",
                  "gated_done", "out_done", "added"))
        LOOPS = NB // 2
        BODY = 2 * SUBS
        IN = (1 + B + B) * 16

        def tokens(t, b, c):
            return t[b, bass.ds(c, 1), :].rearrange("o (t p c) -> p (o t) c", p=128, c=S)

        x1v = x1.rearrange("b (c r) n -> b c (r n)", r=WS)
        ov = out.rearrange("b (c r) n -> b c (r n)", r=WS)
        zv = z.rearrange("(j p) b (c n) -> b p j c n", p=DD, n=WS * S)

        with nc.Block() as block:
            @block.sync
            def _(sp):
                def load(i, c):
                    yield yt[i][:, :, :, :].rearrange("p j b n -> p j (b n)"), ysum[:, :, bass.ds(c, 1), :, :].rearrange(
                        "p j o b n -> p j (o b n)")
                    for b in range(B):
                        yield zt[i][b * DD:(b + 1) * DD, :, :], zv[b, :, :, bass.ds(c, 1), :].rearrange("p j o n -> p j (o n)")
                        yield rt[i][:, b, :, :], tokens(x1v, b, c)

                sp.sem_inc(ready, 1)
                for i in range(2):
                    for dst, src in load(i, i):
                        sp.dma_start(dst, src).then_inc(c_in[i], 16)

                def two(it, last):
                    for i in range(2):
                        c = 2 * it + i if last else sp.snap(2 * it + i)
                        sp.wait_ge(ready, 1)
                        sp.wait_ge(added, (2 * it + i + 1) * SUBS)
                        for b in range(B):
                            sp.dma_start(tokens(ov, b, c), rt[i][:, b, :, :]).then_inc(r_out[i], 16)
                        if not last:
                            n = sp.snap(2 * it + i + 2)
                            sp.wait_ge(ready, 1)
                            sp.wait_ge(r_out[i], it * (B * 16) + B * 16)
                            for dst, src in load(i, n):
                                sp.dma_start(dst, src).then_inc(c_in[i], 16)

                with sp.Fori(0, LOOPS - 1) as it:
                    two(it, False)
                two(LOOPS - 1, True)
                for i in range(2):
                    sp.wait_ge(r_out[i], LOOPS * B * 16)

            def flow(eng, front, back):
                front(0, 0)

                def body(it, last):
                    for q in range(BODY):
                        if not (last and q == BODY - 1):
                            front(it, q + 1) if q < BODY - 1 else front(it + 1, 0)
                        back(it, q)

                with eng.Fori(0, LOOPS - 1) as it:
                    body(it, False)
                body(LOOPS - 1, True)

            def lines(i, j, q):
                return yt[i][:, j].rearrange("p b (h w) -> p h b w", w=WS)[:, 2 * (q % SUBS):2 * (q % SUBS) + 2]

            def grid(ap):
                return ap.rearrange("p (h b w) -> p h b w", h=2, w=WS)

            def later(s):
                return not (isinstance(s, int) and s < 1)

            @block.tensor
            def _(pe):
                pe.wait_ge(ready, 1)

                def front(it, q):
                    s = it * BODY + q
                    if q % SUBS == 0:
                        pe.wait_ge(c_in[q // SUBS], it * IN + IN)
                    if later(s):
                        pe.wait_ge(yc_done, s)
                    for j in range(NJ):
                        mm = pe.matmul(mean_b[:, 0:LINE], mean_of[:, :], lines(q // SUBS, j, q),
                                       start=j == 0, stop=j == NJ - 1)
                    mm.then_inc(mean_done, 1)
                    pe.wait_ge(sq_done, s + 1)
                    if later(s):
                        pe.wait_ge(sd_done, s)
                    for j in range(NJ):
                        mm = pe.matmul(var_b[:, 0:LINE], mean_of[:, :], sq[q % 2][:, j, :],
                                       start=j == 0, stop=j == NJ - 1)
                    mm.then_inc(var_done, 1)

                def back(it, q):
                    s = it * BODY + q
                    pe.wait_ge(gated_done, s + 1)
                    if later(s):
                        pe.wait_ge(added, s)
                    for t in range(T3):
                        for b in range(B):
                            rows = slice(b * DD, (b + 1) * DD)
                            for j in range(NJ):
                                mm = pe.matmul(out_b[t][b][:, 0:S], gated[q % 2][rows, j, t * 128:(t + 1) * 128],
                                               wo[rows, j, :], start=j == 0, stop=j == NJ - 1)
                    mm.then_inc(out_done, 1)

                flow(pe, front, back)

            @block.vector
            def _(dve):
                dve.wait_ge(ready, 1)

                def front(it, q):
                    s = it * BODY + q
                    dve.wait_ge(mean_done, s + 1)
                    for j in range(NJ):
                        m = dve.tensor_tensor(grid(yc[q % 2][:, j, :]), lines(q // SUBS, j, q),
                                              grid(mean_b[:, 0:LINE]), ALU.subtract)
                    m.then_inc(yc_done, 1)
                    dve.wait_ge(sd_done, s + 1)
                    dve.reciprocal(sd[q % 2][:, :], sd[q % 2][:, :]).then_inc(inv_done, 1)

                def back(it, q):
                    i, s = q // SUBS, it * BODY + q
                    dve.wait_ge(inv_done, s + 1)
                    dve.tensor_tensor(yc[q % 2][:, :, :], yc[q % 2][:, :, :],
                                      sd[q % 2][:, :].rearrange("p (o t) -> p o t", o=1).broadcast_to([128, NJ, LINE]),
                                      ALU.mult).then_inc(scaled, 1)
                    dve.wait_ge(out_done, s + 1)
                    for t in range(T3):
                        for b in range(B):
                            v = rt[i][:, b, T3 * (q % SUBS) + t, :]
                            m = dve.tensor_tensor(v, out_b[t][b][:, 0:S], v, ALU.add)
                    m.then_inc(added, 1)

                flow(dve, front, back)

            @block.scalar
            def _(act):
                act.wait_ge(ready, 1)

                def front(it, q):
                    s = it * BODY + q
                    act.wait_ge(yc_done, s + 1)
                    act.activation(sq[q % 2][:, :, :], yc[q % 2][:, :, :], ACT.Square).then_inc(sq_done, 1)
                    act.wait_ge(var_done, s + 1)
                    act.activation(sd[q % 2][:, :], var_b[:, 0:LINE], ACT.Sqrt, bias=epst[:, 0:1]).then_inc(sd_done, 1)

                def back(it, q):
                    s = it * BODY + q
                    act.wait_ge(scaled, s + 1)
                    for j in range(NJ):
                        m = act.activation(sq[q % 2][:, j, :], yc[q % 2][:, j, :], ACT.Identity,
                                           scale=lnw[:, j:j + 1], bias=lnb[:, j:j + 1])
                    m.then_inc(shifted, 1)

                flow(act, front, back)

            @block.gpsimd
            def _(pool):
                pool.wait_ge(ready, 1)

                def back(it, q):
                    i, s = q // SUBS, it * BODY + q
                    pool.wait_ge(shifted, s + 1)
                    if q % SUBS == 0:
                        pool.wait_ge(c_in[i], it * IN + IN)
                    if later(s):
                        pool.wait_ge(out_done, s)
                    pool.tensor_tensor(gated[q % 2][:, :, :], sq[q % 2][:, :, :],
                                       zt[i][:, :, (q % SUBS) * LINE:(q % SUBS + 1) * LINE], ALU.mult).then_inc(gated_done, 1)

                flow(pool, lambda it, q: None, back)


def scan_phase(nc, xc, ysum, x_proj_w, dt_projs_w, dt_projs_b, A_logs, Ds, directions=range(K)):
    with ExitStack() as ctx:
        def sb(name, shape, dt=F32):
            return ctx.enter_context(nc.sbuf_tensor(name, shape, dt))

        def sem(name):
            return ctx.enter_context(nc.semaphore(name))

        u = [sb(f"u{i}", [128, NJ, NB, BLK]) for i in range(2)]
        yt = [sb(f"yt{i}", [128, NJ, NB, BLK]) for i in range(2)]
        decay = [sb(f"decay{i}", [128, NJ, LINE]) for i in range(4)]
        drive = [sb(f"drive{i}", [128, NJ, LINE]) for i in range(2)]
        state = [sb(f"state{i}", [128, NJ, LINE]) for i in range(2)]
        prod = [sb(f"prod{i}", [128, NJ, LINE]) for i in range(2)]
        cb = [sb(f"cb{i}", [128, LINE]) for i in range(2)]
        delta = [sb(f"delta{i}", [128, NJ, LINE]) for i in range(2)]
        du = [sb(f"du{i}", [128, NJ, LINE]) for i in range(2)]
        tail = sb("tail", [128, NJ, LINE])
        low = sb("low", [128, NJ, LINE])
        quad = sb("quad", [128, NJ, LINE])
        high = sb("high", [128, NJ, LINE])
        ln_one = sb("ln_one", [128, 2])
        consts = sb("consts", [128, 2])
        relu = sb("relu", [128, NJ, LINE])
        bc3 = [sb(f"bc3_{i}", [3 * NBC, LINE], BF16) for i in range(2)]
        rest = sb("rest", [2 * NBC, LINE])
        dts = sb("dts", [XR + 1, LINE])
        carry = sb("carry", [128, N, NJ])
        ident = sb("ident", [128, 128])
        sel = sb("sel", [3 * NBC, 2, N, B, DD], BF16)
        xpw = sb("xpw", [128, K, NJ, XR])
        dtw = sb("dtw", [XR + 1, K, NJ, 128])
        a_neg = sb("a_neg", [128, K * NJ, N])
        a_exp = sb("a_exp", [128, K * NJ, N])
        ds_t = sb("ds_t", [128, K * NJ])
        dsum = sb("dsum", [128, NJ])

        ybank = ctx.enter_context(nc.psum_tensor("ybank", [128, NJ, 512], F32))
        bbank = ctx.enter_context(nc.psum_tensor("bbank", [128, 2, 512], F32))
        cbank = ctx.enter_context(nc.psum_tensor("cbank", [128, 512], F32))
        pbank = ctx.enter_context(nc.psum_tensor("pbank", [128, 2, 512], F32))

        w_zero, w_in, w_set, w_exp, w_one = sem("w_zero"), sem("w_in"), sem("w_set"), sem("w_exp"), sem("w_one")
        n_in = [0]
        with nc.Block() as block:
            @block.gpsimd
            def _(pool):
                pool.memset(ident[:, :], 0.0).then_inc(w_zero, 1)
                pool.memset(sel[:, :, :, :, :], 0.0).then_inc(w_zero, 1)
                pool.memset(xpw[:, :, :, :], 0.0).then_inc(w_zero, 1)
                pool.memset(dtw[:, :, :, :], 0.0).then_inc(w_zero, 1)
                pool.memset(dts[:, :], 1.0).then_inc(w_zero, 1)
                pool.wait_ge(w_zero, 5)
                pool.affine_select(out=ident[:, :], in_=ident[:, :], compare_op=ALU.not_equal, fill=1.0,
                                   base=0, pattern=[[-1, 128]], channel_multiplier=1).then_inc(w_set, 1)
                done = 1
                for part in range(3):
                    for w in range(2):
                        pool.wait_ge(w_set, done)
                        pool.affine_select(out=sel[:, w], in_=sel[:, w], compare_op=ALU.not_equal,
                                           fill=1.0, base=-(NBC * part + B * N * w),
                                           pattern=[[-1, N], [-N, B], [0, DD]],
                                           channel_multiplier=1).then_inc(w_set, 1)
                        done += 1

            @block.sync
            def _(sp):
                sp.wait_ge(w_zero, 5)
                with nc.allow_non_contiguous_dma("weights, once"):
                    for b in range(B):
                        rows = slice(b * DD, (b + 1) * DD)
                        for j in range(NJ):
                            for k in range(K):
                                w = x_proj_w[k, :, j * DD:(j + 1) * DD].rearrange("c p -> p c")
                                for lo, n, to in ((R, N, b * N), (R + N, N, B * N + b * N), (0, R, NBC + b * R)):
                                    sp.dma_start(xpw[rows, k, j, to:to + n], w[:, lo:lo + n]).then_inc(w_in, 16)
                                    n_in[0] += 16
                        for k in range(K):
                            for j in range(NJ):
                                sp.dma_start(dtw[NBC + b * R:NBC + (b + 1) * R, k, j, rows],
                                             dt_projs_w[k, j * DD:(j + 1) * DD, :].rearrange("p r -> r p")
                                             ).then_inc(w_in, 16)
                                n_in[0] += 16
                        sp.dma_start(dtw[XR:XR + 1, :, :, rows].rearrange("o k j p -> o (k j) p"),
                                     dt_projs_b.rearrange("(o k) (j p) -> o (k j) p", o=1, p=DD)).then_inc(w_in, 16)
                        sp.dma_start(a_exp[rows, :, :],
                                     A_logs.rearrange("k (j p) n -> p (k j) n", p=DD)).then_inc(w_in, 16)
                        sp.dma_start(ds_t[rows, :], Ds.rearrange("k (j p) -> p (k j)", p=DD)).then_inc(w_in, 16)
                        n_in[0] += 48
                sp.wait_ge(w_in, n_in[0])

            @block.scalar
            def _(act):
                act.wait_ge(w_in, n_in[0])
                act.preload_act_table_set("natural_log_exp_and_others")
                act.activation(a_exp[:, :, :], a_exp[:, :, :], ACT.Exp).then_inc(w_exp, 1)
                act.wait_ge(w_one, 1)
                act.activation(ln_one[:, 0:1], ln_one[:, 0:1], ACT.Ln).then_inc(w_exp, 1)

            @block.vector
            def _(dve):
                dve.memset(consts[:, 0:1], -SPLIT)
                dve.memset(consts[:, 1:2], C1 / (2 * C2 ** 0.5))
                dve.memset(ln_one[:, :], 1.0).then_inc(w_one, 1)
                dve.wait_ge(w_exp, 2)
                dve.tensor_scalar(ln_one[:, 1:2], ln_one[:, 0:1], -1.0, None, ALU.mult)
                dve.tensor_scalar(a_neg[:, :, :], a_exp[:, :, :], -1.0, None, ALU.mult)
                dve.tensor_reduce(dsum[:, :], ds_t[:, :].rearrange("p (k j) -> p j k", j=NJ),
                                  mybir.AxisListType.X, ALU.add)

        def lines(tile, j, col, first):
            if col:
                return tile[:, j].rearrange("p b (h w) -> p w b h", w=WS)[:, first:first + 2]
            return tile[:, j].rearrange("p b (h w) -> p h b w", w=WS)[:, first:first + 2]

        NPAIR = NB // 2
        QS = 2 * SUBS

        def later(s):
            return not (isinstance(s, int) and s == 0)

        ready = sem("ready")
        sp_waited = sem("sp_waited")
        u_in = [sem(f"u_in{i}") for i in range(2)]
        y_in = [sem(f"y_in{i}") for i in range(2)]
        y_out = [sem(f"y_out{i}") for i in range(2)]
        xp_done, dt_ready, bc_hi, bc_rest, bc_mid, bc_ready = map(
            sem, ("xp_done", "dt_ready", "bc_hi", "bc_rest", "bc_mid", "bc_ready"))
        dt_done, dt_taken, soft_ready, delta_ready, du_ready = map(
            sem, ("dt_done", "dt_taken", "soft_ready", "delta_ready", "du_ready"))
        high_ready, low_ready, quad_ready, log_low, log_ready = map(
            sem, ("high_ready", "low_ready", "quad_ready", "log_low", "log_ready"))
        b_ready, c_ready, c_copied, decay_ready = map(sem, ("b_ready", "c_ready", "c_copied", "decay_ready"))
        drive_done, scan_done, prod_done, carry_done, acc_done, y_done = map(
            sem, ("drive_done", "scan_done", "prod_done", "carry_done", "acc_done", "y_done"))

        for turn, k in enumerate(directions):
            col, rev = k % 2 == 1, k >= 2

            def chunk(c):
                return NB - 1 - c if rev else c

            def first_line(q):
                return (WS - 2 - 2 * (q % SUBS)) if rev else 2 * (q % SUBS)

            def at(it, q):
                return (it + turn * NPAIR) * QS + q

            def tiles(it):
                return (it + turn * NPAIR) * 16

            def part(t, c):
                c = bass.ds(c, 1)
                return (t[:, :, :, c, :] if col else t[:, :, c, :, :]).rearrange("p j a b n -> p j (a b) n")

            with nc.Block() as block:
                @block.sync
                def _(sp):
                    def wait(s, v):
                        sp.wait_ge(s, v)
                        sp.sem_inc(sp_waited, 1)

                    sp.wait_ge(ready, turn + 1)
                    for i in range(2):
                        sp.dma_start(u[i][:, :, :, :], part(xc, chunk(i))).then_inc(u_in[i], 16)
                        if k != directions[0]:
                            sp.dma_start(yt[i][:, :, :, :], part(ysum, chunk(i))).then_inc(y_in[i], 16)

                    def chunk_pair(it, last):
                        for i in range(2):
                            here = sp.snap(chunk(2 * it + i)) if not last else chunk(2 * it + i)
                            wait(y_done, at(it, (i + 1) * SUBS))
                            sp.dma_start(part(ysum, here), yt[i][:, :, :, :]).then_inc(y_out[i], 16)
                            if not last:
                                after = sp.snap(chunk(2 * it + i + 2))
                                sp.dma_start(u[i][:, :, :, :], part(xc, after)).then_inc(u_in[i], 16)
                                if k != directions[0]:
                                    wait(y_out[i], tiles(it + 1))
                                    sp.dma_start(yt[i][:, :, :, :], part(ysum, after)).then_inc(y_in[i], 16)

                    with sp.Fori(0, NPAIR - 1) as it:
                        chunk_pair(it, False)
                    chunk_pair(NPAIR - 1, True)
                    for i in range(2):
                        sp.wait_ge(y_out[i], tiles(NPAIR))

                def pairs(eng, body):
                    with eng.Fori(0, NPAIR - 1) as it:
                        body(it, False)
                    body(NPAIR - 1, True)

                @block.tensor
                def _(pe):
                    def x_proj(it, q):
                        s = at(it, q)
                        if q % SUBS == 0:
                            pe.wait_ge(u_in[q // SUBS % 2], tiles(it + 1))
                        if later(s):
                            pe.wait_ge(dt_taken, s * NJ)
                        for j in range(NJ):
                            mm = pe.matmul(pbank[0:XR, 0, 0:LINE], xpw[:, k, j, :],
                                           lines(u[q // SUBS % 2], j, col, first_line(q)),
                                           start=j == 0, stop=j == NJ - 1)
                        mm.then_inc(xp_done, 1)

                    def step_size(it, q, j):
                        s = at(it, q)
                        if j == 0:
                            pe.wait_ge(dt_ready, s + 1)
                        if j == 1:
                            pe.wait_ge(bc_rest, s + 1)
                        if j == 2 or (j == 0 and later(s)):
                            pe.wait_ge(dt_taken, s * NJ + j // 2)
                        pe.matmul(pbank[:, (j + 1) % 2, 0:LINE], dtw[NBC:XR + 1, k, j, :], dts[NBC:XR + 1, :],
                                  start=True, stop=True).then_inc(dt_done, 1)

                    def spread(it, q, n):
                        g = at(it, q) * N + n
                        if n == 0:
                            pe.wait_ge(bc_ready, at(it, q) + 1)
                        pe.wait_ge(drive_done, g + 1)
                        pe.matmul(bbank[:, n % 2, 0:LINE], sel[:, 0, n].rearrange("r b d -> r (b d)"),
                                  bc3[q % 2][:, :], start=True, stop=True).then_inc(b_ready, 1)
                        if later(g):
                            pe.wait_ge(c_copied, g)
                        pe.matmul(cbank[:, 0:LINE], sel[:, 1, n].rearrange("r b d -> r (b d)"),
                                  bc3[q % 2][:, :], start=True, stop=True).then_inc(c_ready, 1)

                    def add_up(it, q, n):
                        g = at(it, q) * N + n
                        pe.wait_ge(prod_done, g + 3)
                        if n == 0:
                            if later(at(it, q)):
                                pe.wait_ge(y_done, at(it, q))
                        for j in range(NJ):
                            mm = pe.matmul(ybank[:, j, 0:LINE], ident[:, :], prod[n % 2][:, j, :],
                                           start=n == 0, stop=n == N - 1)
                        mm.then_inc(acc_done, 1)

                    pe.wait_ge(ready, turn + 1)
                    x_proj(0, 0)
                    for j in range(NJ):
                        step_size(0, 0, j)
                    spread(0, 0, 0)

                    def body(it, last):
                        for q in range(QS):
                            end = last and q == QS - 1
                            nit, nq = (it, q + 1) if q < QS - 1 else (it + 1, 0)
                            for n in range(N):
                                if n < N - 1:
                                    spread(it, q, n + 1)
                                if n == 0 and not end:
                                    x_proj(nit, nq)
                                if 1 <= n <= NJ and not end:
                                    step_size(nit, nq, n - 1)
                                if n == N - 1 and not end:
                                    spread(nit, nq, 0)
                                if n:
                                    add_up(it, q, n - 1)
                            add_up(it, q, N - 1)

                    pairs(pe, body)

                @block.scalar
                def _(act):
                    def front(it, q):
                        s = at(it, q)
                        act.wait_ge(xp_done, s + 1)
                        act.activation(bc3[q % 2][0:NBC, :], pbank[0:NBC, 0, 0:LINE], ACT.Copy).then_inc(bc_hi, 1)
                        act.activation(dts[NBC:XR, :], pbank[NBC:XR, 0, 0:LINE], ACT.Copy).then_inc(dt_ready, 1)

                    def middle(it, q):
                        act.wait_ge(bc_rest, at(it, q) + 1)
                        act.activation(bc3[q % 2][NBC:2 * NBC, :], rest[NBC:2 * NBC, :], ACT.Copy).then_inc(bc_mid, 1)

                    def take(it, q, j):
                        s = at(it, q)
                        if j == 0 and later(s):
                            act.wait_ge(delta_ready, s)
                        act.wait_ge(dt_done, s * NJ + j + 1)
                        act.activation(tail[:, j, :], pbank[:, (j + 1) % 2, 0:LINE], ACT.Abs)
                        act.activation(relu[:, j, :], pbank[:, (j + 1) % 2, 0:LINE], ACT.Relu).then_inc(dt_taken, 1)

                    def soft_exp(it, q):
                        s = at(it, q)
                        act.wait_ge(dt_taken, (s + 1) * NJ)
                        act.activation(tail[:, :, :], tail[:, :, :], ACT.Exp, scale=-1.0).then_inc(soft_ready, 1)
                        act.wait_ge(soft_ready, 2 * s + 1)
                        act.activation(high[:, :, :], tail[:, :, :], ACT.Relu, bias=consts[:, 0:1]).then_inc(high_ready, 1)

                    def soft_ln(it, q):
                        s = at(it, q)
                        act.wait_ge(low_ready, s + 1)
                        act.activation(quad[:, :, :], low[:, :, :], ACT.Square, scale=C2 ** 0.5,
                                       bias=consts[:, 1:2]).then_inc(quad_ready, 1)
                        act.wait_ge(high_ready, s + 1)
                        act.activation(high[:, :, :], high[:, :, :], ACT.Ln, scale=1.0 / (1.0 + SPLIT),
                                       bias=1.0).then_inc(soft_ready, 1)

                    act.wait_ge(ready, turn + 1)
                    act.preload_act_table_set("natural_log_exp_and_others")
                    front(0, 0)
                    middle(0, 0)
                    for j in range(NJ):
                        take(0, 0, j)
                    soft_exp(0, 0)
                    soft_ln(0, 0)

                    def body(it, last):
                        for q in range(QS):
                            end = last and q == QS - 1
                            nit, nq = (it, q + 1) if q < QS - 1 else (it + 1, 0)
                            if k == directions[0] and q % SUBS == 0:
                                i = q // SUBS % 2
                                act.wait_ge(u_in[i], tiles(it + 1))
                                act.wait_ge(y_out[i], tiles(it))
                                for j in range(NJ):
                                    m = act.activation(yt[i][:, j], u[i][:, j], ACT.Copy, scale=dsum[:, j:j + 1])
                                m.then_inc(y_in[i], 16)
                            for n in range(N):
                                g = at(it, q) * N + n
                                if n == 0:
                                    act.wait_ge(delta_ready, at(it, q) + 1)
                                act.wait_ge(scan_done, g + 1)
                                for j in range(NJ):
                                    e = act.activation(decay[n % 4][:, j, :], delta[q % 2][:, j, :], ACT.Exp,
                                                       scale=a_neg[:, k * NJ + j, n:n + 1])
                                e.then_inc(decay_ready, 1)
                                act.wait_ge(c_ready, g + 1)
                                act.wait_ge(prod_done, g + 1)
                                act.activation(cb[n % 2][:, :], cbank[:, 0:LINE], ACT.Copy).then_inc(c_copied, 1)
                                if end:
                                    continue
                                if n == 0:
                                    front(nit, nq)
                                if n == 1:
                                    middle(nit, nq)
                                if n == 2:
                                    take(nit, nq, 0)
                                if n == 3:
                                    take(nit, nq, 1)
                                    take(nit, nq, 2)
                                    soft_exp(nit, nq)
                                if n == 4:
                                    soft_ln(nit, nq)

                    pairs(act, body)

                @block.gpsimd
                def _(pool):
                    if turn == 0:
                        pool.sem_inc(carry_done, N)
                        for s in (drive_done, scan_done, prod_done, acc_done):
                            pool.sem_inc(s, 2)
                    pool.memset(carry[:, :, :], 0.0).then_inc(ready, 1)

                    def step_inputs(it, q, n):
                        s = at(it, q)
                        i = q // SUBS % 2
                        if n == 0:
                            pool.wait_ge(log_ready, s + 1)
                            pool.tensor_tensor(delta[q % 2][:, :, :], relu[:, :, :], low[:, :, :],
                                               ALU.add).then_inc(delta_ready, 1)
                        if n == 1:
                            if q % SUBS == 0:
                                pool.wait_ge(u_in[i], tiles(it + 1))
                            pool.wait_ge(delta_ready, s + 1)
                            for j in range(NJ):
                                v = lines(u[i], j, col, first_line(q))
                                m = pool.tensor_tensor(du[q % 2][:, j, :].rearrange("p (l a b) -> p l a b", l=2, b=WS),
                                                       delta[q % 2][:, j, :].rearrange("p (l a b) -> p l a b", l=2, b=WS),
                                                       v, ALU.mult)
                            m.then_inc(du_ready, 1)

                    for n in range(2):
                        step_inputs(0, 0, n)
                    edge = 0 if rev else LINE - 1

                    def body(it, last):
                        for q in range(QS):
                            end = last and q == QS - 1
                            nit, nq = (it, q + 1) if q < QS - 1 else (it + 1, 0)
                            for n in range(N):
                                g = at(it, q) * N + n
                                if n >= N - 2 and not end:
                                    step_inputs(nit, nq, n - (N - 2))
                                pool.wait_ge(scan_done, g + 3)
                                pool.wait_ge(c_copied, g + 1)
                                pool.wait_ge(acc_done, g + 1)
                                pool.tensor_tensor(prod[n % 2][:, :, :], state[n % 2][:, :, :],
                                                   cb[n % 2][:, :].rearrange("p (o t) -> p o t", o=1).broadcast_to([128, NJ, LINE]),
                                                   ALU.mult).then_inc(prod_done, 1)
                                pool.tensor_copy(carry[:, n, :], state[n % 2][:, :, edge]).then_inc(carry_done, 1)

                    pairs(pool, body)

                @block.vector
                def _(dve):
                    dve.wait_ge(ready, turn + 1)

                    def split(it, q):
                        s = at(it, q)
                        dve.wait_ge(bc_hi, s + 1)
                        dve.tensor_tensor(rest[NBC:2 * NBC, :], pbank[0:NBC, 0, 0:LINE], bc3[q % 2][0:NBC, :],
                                          ALU.subtract).then_inc(bc_rest, 1)

                    def split_low(it, q):
                        dve.wait_ge(bc_mid, at(it, q) + 1)
                        dve.tensor_tensor(bc3[q % 2][2 * NBC:3 * NBC, :], rest[NBC:2 * NBC, :],
                                          bc3[q % 2][NBC:2 * NBC, :], ALU.subtract).then_inc(bc_ready, 1)

                    def soft_low(it, q):
                        s = at(it, q)
                        dve.wait_ge(soft_ready, 2 * s + 1)
                        if later(s):
                            dve.wait_ge(delta_ready, s)
                        dve.tensor_scalar(low[:, :, :], tail[:, :, :], SPLIT, None, ALU.min).then_inc(low_ready, 1)

                    def soft_sum(it, q):
                        s = at(it, q)
                        dve.wait_ge(quad_ready, s + 1)
                        dve.scalar_tensor_tensor(out=low[:, :, :], in0=quad[:, :, :], scalar=C0 - C1 * C1 / (4 * C2),
                                                 in1=low[:, :, :], op0=ALU.add, op1=ALU.mult).then_inc(log_low, 1)
                        dve.wait_ge(soft_ready, 2 * s + 2)
                        dve.wait_ge(log_low, s + 1)
                        dve.scalar_tensor_tensor(out=low[:, :, :], in0=high[:, :, :], scalar=ln_one[:, 1:2],
                                                 in1=low[:, :, :], op0=ALU.add, op1=ALU.add).then_inc(log_ready, 1)

                    split(0, 0)
                    split_low(0, 0)
                    soft_low(0, 0)
                    soft_sum(0, 0)

                    def drive_in(it, q, n):
                        g = at(it, q) * N + n
                        if n == 0:
                            dve.wait_ge(du_ready, at(it, q) + 1)
                        dve.wait_ge(b_ready, g + 1)
                        dve.wait_ge(scan_done, g + 1)
                        dve.tensor_tensor(drive[n % 2][:, :, :], du[q % 2][:, :, :],
                                          bbank[:, n % 2:n % 2 + 1, 0:LINE].broadcast_to([128, NJ, LINE]),
                                          ALU.mult).then_inc(drive_done, 1)

                    def scans(it, q, n):
                        g = at(it, q) * N + n
                        dve.wait_ge(decay_ready, g + 1)
                        dve.wait_ge(drive_done, g + 3)
                        dve.wait_ge(carry_done, g + N - 1)
                        for j in range(NJ):
                            tt = lambda t: t[:, j, ::-1] if rev else t[:, j, :]
                            sc = dve.tensor_tensor_scan(out=tt(state[n % 2]), data0=tt(decay[n % 4]),
                                                        data1=tt(drive[n % 2]), initial=carry[:, n, j:j + 1],
                                                        op0=ALU.mult, op1=ALU.add)
                        sc.then_inc(scan_done, 1)

                    def take_y(it, q):
                        i = q // SUBS % 2
                        if q % SUBS == 0:
                            dve.wait_ge(y_in[i], tiles(it + 1))
                        dve.wait_ge(acc_done, (at(it, q) + 1) * N + 2)
                        for j in range(NJ):
                            v = lines(yt[i], j, col, first_line(q))
                            ad = dve.tensor_tensor(v, ybank[:, j, 0:LINE].rearrange("p (l a b) -> p l a b", l=2, b=WS),
                                                   v, ALU.add)
                        ad.then_inc(y_done, 1)

                    def body(it, last):
                        for q in range(QS):
                            end = last and q == QS - 1
                            nit, nq = (it, q + 1) if q < QS - 1 else (it + 1, 0)
                            drive_in(it, q, 0)
                            for n in range(N):
                                if n < N - 1:
                                    drive_in(it, q, n + 1)
                                scans(it, q, n)
                                if n == 0 and q:
                                    take_y(it, q - 1)
                                if n == 1 and not end:
                                    split(nit, nq)
                                if n == 2 and not end:
                                    split_low(nit, nq)
                                if n == 3 and not end:
                                    soft_low(nit, nq)
                                if n == 4 and not end:
                                    soft_sum(nit, nq)
                        take_y(it, QS - 1)

                    pairs(dve, body)


def build(nc, x, Wq, bq, Wk, bk, Wv, bv, Wskip, bskip, in_w_t, conv_w, conv_b, x_proj_w, dt_projs_w, dt_projs_b,
          A_logs, Ds, ln_w, ln_b, out_w_t, out):
    def scratch(name, shape):
        return nc.dram_tensor(name, shape, F32, kind="Internal").ap()

    stats0, stats1 = scratch("stats0", (B, 2, S)), scratch("stats1", (B, 2, S))
    x1 = scratch("x1", (B, S, S * S))
    xf = scratch("xf", (S, B, S + 2, S))
    z = scratch("z", (S, B, S * S))
    xc = scratch("xc", (128, NJ, NB, NB, BLK))
    ysum = scratch("ysum", (128, NJ, NB, NB, BLK))
    stats_phase(nc, "s0_", x, stats0, GN_EPS)
    attention_phase(nc, x.rearrange("c b (s n) -> c (b s) n", s=NW), stats0, Wq, bq, Wk, bk, Wv, bv, Wskip, bskip, x1)
    stats_phase(nc, "s1_", x1.rearrange("b c n -> c b n"), stats1, GN_EPS)
    project_phase(nc, x1, stats1, in_w_t, xf, z)
    conv_phase(nc, xf, conv_w, conv_b, xc)
    scan_phase(nc, xc, ysum, x_proj_w, dt_projs_w, dt_projs_b, A_logs, Ds)
    final_phase(nc, ysum, z, x1, ln_w, ln_b, out_w_t, out)


def kernel(x, **w):
    import concourse.bacc as bacc
    import numpy as np
    from concourse.bass_utils import run_bass_kernel_spmd

    def plain(name):
        return np.asarray(w[name])

    arrays = {"x": np.asarray(x).transpose(1, 0, 2, 3).reshape(S, B, S * S)}
    for n in ("Wq", "bq", "Wk", "bk", "Wv", "bv", "Wskip", "bskip"):
        arrays[n] = plain("L0_conv_" + n)
    arrays["in_w_t"] = plain("L1_conv_in_proj_w").T
    arrays["conv_w"] = plain("L1_conv_conv_w").reshape(S, 9)
    arrays["conv_b"] = plain("L1_conv_conv_b")
    for n in ("x_proj_w", "dt_projs_w", "dt_projs_b", "A_logs", "Ds", "ln_w", "ln_b"):
        arrays[n] = plain("L1_conv_" + n)
    arrays["out_w_t"] = plain("L1_conv_out_proj_w").T
    arrays = {n: np.ascontiguousarray(a) for n, a in arrays.items()}
    nc = bacc.Bacc("TRN2", target_bir_lowering=False, num_devices=1)
    args = [nc.dram_tensor(n, a.shape, F32, kind="ExternalInput").ap() for n, a in arrays.items()]
    out = nc.dram_tensor("out", (B, S, S * S), F32, kind="ExternalOutput").ap()
    build(nc, *args, out)
    got = run_bass_kernel_spmd(nc, [arrays], core_ids=[0]).results[0]["out"]
    return got.reshape(B, S, S, S)
```

```python
from contextlib import ExitStack

import concourse.bass as bass
from concourse import mybir

F32 = mybir.dt.float32
BF16 = mybir.dt.bfloat16
ALU = mybir.AluOpType
ACT = mybir.ActivationFunctionType
AX = mybir.AxisListType

B = 2
S = 192
HALF = S // 2
GROUPS = 32
GW = S // GROUPS

WS = 8
NW = S // WS
TOK = WS * WS
PAIR = 2 * TOK
HEADS = 8
DH = S // HEADS
STRIPS = B * NW
PAIRS = NW // 2
QUADS = PAIRS // 4
FAR = -5e8
GUARD = -2e38
TAKEN = -3e38
OFF = -1e30
DD = 64
NJ = S // DD
NB = S // WS
BLK = WS * WS
LINE = 2 * S
SUBS = WS // 2
LN_EPS = 1e-5
K = 4
N = 8
R = 12
NBC = 2 * B * N
XR = NBC + B * R
SPLIT = 1 / 64
C0, C1, C2 = 0.9999999708, -0.49996632, 0.327558
GN_EPS = 1e-5


def stats_phase(nc, tag, x, stats, eps, st=None):
    ROWS = 64
    T = S // ROWS
    CH = B * T if st is None else st.shape[2] // B
    with ExitStack() as ctx:
        def sb(name, shape, dt=F32):
            return ctx.enter_context(nc.sbuf_tensor(tag + name, shape, dt))

        def sem(name):
            return ctx.enter_context(nc.semaphore(tag + name))

        if st is None:
            xt = [sb(f"xt{i}", [HALF, ROWS, S]) for i in range(2)]
            st = sb("st", [HALF, GROUPS, 2 * CH, 6])
            xv = x.rearrange("(a p) b (t n) -> a b p t n", a=2, t=T)
        mv = sb("mv", [HALF, B * GROUPS, 2])
        mean_of = sb("mean_of", [HALF, HALF])
        tot = sb("tot", [HALF, B, GROUPS, 2])
        dev = sb("dev", [HALF, B * GROUPS])
        dev2 = sb("dev2", [HALF, B * GROUPS])
        var = sb("var", [HALF, B * GROUPS])
        sd = sb("sd", [HALF, B * GROUPS])
        rs = sb("rs", [HALF, B, GROUPS])
        wide = sb("wide", [HALF, B, 2, GROUPS, GW])
        epst = sb("epst", [HALF, 1])
        ps = ctx.enter_context(nc.psum_tensor(tag + "ps", [HALF, 2, 512], F32))
        x_in = [sem(f"x_in{i}") for i in range(2)]
        chunk_done, aggr, ones_set, summed, chain, rooted, stored = map(
            sem, ("chunk_done", "aggr", "ones_set", "summed", "chain", "rooted", "stored"))
        with nc.Block() as block:
            @block.sync
            def _(sp):
                for b in range(B if x is not None else 0):
                    with sp.Fori(0, T) as t:
                        for i in range(2):
                            src = xv[i, b, :, bass.ds(t, 1), :].rearrange("p o n -> p (o n)")
                            sp.wait_ge(ones_set, 1)
                            sp.wait_ge(chunk_done, (t + b * T) * 2 + i + 1)
                            sp.dma_start(xt[i][:, :, :].rearrange("p r w -> p (r w)"), src).then_inc(x_in[i], 16)
                sp.wait_ge(chain, 13)
                sp.dma_start(stats.rearrange("(o b) s w -> o (b s w)", o=1),
                             wide[0:1].rearrange("o b s g w -> o (b s g w)")).then_inc(stored, 16)
                sp.wait_ge(stored, 16)

            @block.vector
            def _(dve):
                dve.memset(mean_of[:, :], 1.0 / HALF)
                dve.memset(epst[:, :], eps).then_inc(ones_set, 1)
                if x is not None:
                    dve.sem_inc(chunk_done, 2)
                    with dve.Fori(0, CH) as c:
                        for i in range(2):
                            dve.wait_ge(x_in[i], c * 16 + 16)
                            for g in range(GROUPS):
                                b = dve.bn_stats(st[:, g, bass.ds(2 * c + i, 1), :].rearrange("p o s -> p (o s)"),
                                                 xt[i][:, :, g * GW:(g + 1) * GW])
                            b.then_inc(chunk_done, 1)
                    dve.wait_ge(chunk_done, 2 * CH + 2)
                for b in range(B):
                    for g in range(GROUPS):
                        a = dve.bn_aggr(mv[:, b * GROUPS + g, :],
                                        st[:, g, b * CH:(b + 1) * CH, :].rearrange("p c s -> p (c s)"))
                a.then_inc(aggr, 1)
                dve.wait_ge(summed, 1)
                dve.tensor_copy(tot[:, :, :, :].rearrange("p b g s -> p (b g s)"), ps[:, 0, 0:2 * B * GROUPS]).then_inc(chain, 1)
                dve.wait_ge(chain, 1)
                mean = tot[:, :, :, 0].rearrange("p b g -> p (b g)")
                dve.tensor_tensor(dev[:, :], mv[:, :, 0], mean, ALU.subtract).then_inc(chain, 1)
                dve.wait_ge(chain, 2)
                dve.tensor_tensor(dev2[:, :], dev[:, :], dev[:, :], ALU.mult).then_inc(chain, 1)
                dve.wait_ge(summed, 2)
                dve.tensor_tensor(var[:, :], ps[:, 1, 0:B * GROUPS], tot[:, :, :, 1].rearrange("p b g -> p (b g)"),
                                  ALU.add).then_inc(chain, 1)
                dve.wait_ge(rooted, 1)
                r = rs[:, :, :].rearrange("p b g -> p (b g)")
                dve.reciprocal(r, sd[:, :]).then_inc(chain, 1)
                dve.wait_ge(chain, 5)
                dve.tensor_tensor(dev[:, :], r, r, ALU.mult).then_inc(chain, 1)
                dve.wait_ge(chain, 6)
                dve.scalar_tensor_tensor(out=dev[:, :], in0=var[:, :], scalar=eps, in1=dev[:, :],
                                         op0=ALU.add, op1=ALU.mult).then_inc(chain, 1)
                dve.wait_ge(chain, 7)
                dve.tensor_scalar(dev[:, :], dev[:, :], -0.5, 1.5, ALU.mult, ALU.add).then_inc(chain, 1)
                dve.wait_ge(chain, 8)
                dve.tensor_tensor(r, r, dev[:, :], ALU.mult).then_inc(chain, 1)
                dve.wait_ge(chain, 9)
                for b in range(B):
                    dve.tensor_copy(wide[:, b, 0], tot[:, b, :, 0:1].broadcast_to([HALF, GROUPS, GW])).then_inc(chain, 1)
                    dve.tensor_copy(wide[:, b, 1], rs[:, b, :].rearrange("p (g o) -> p g o", o=1)
                                    .broadcast_to([HALF, GROUPS, GW])).then_inc(chain, 1)

            @block.tensor
            def _(pe):
                pe.wait_ge(aggr, 1)
                pe.matmul(ps[:, 0, 0:2 * B * GROUPS], mean_of[:, :], mv[:, :, :].rearrange("p g s -> p (g s)"),
                          start=True, stop=True).then_inc(summed, 1)
                pe.wait_ge(chain, 3)
                pe.matmul(ps[:, 1, 0:B * GROUPS], mean_of[:, :], dev2[:, :], start=True, stop=True).then_inc(summed, 1)

            @block.scalar
            def _(act):
                act.wait_ge(chain, 4)
                act.activation(sd[:, :], var[:, :], ACT.Sqrt, bias=epst[:, 0:1]).then_inc(rooted, 1)


def attention_phase(nc, x, stats, Wq, bq, Wk, bk, Wv, bv, Ws, bs, x1, st):
    with ExitStack() as ctx:
        def sb(name, shape, dt=F32):
            return ctx.enter_context(nc.sbuf_tensor("a_" + name, shape, dt))

        def sem(name):
            return ctx.enter_context(nc.semaphore("a_" + name))

        def bank(name):
            return ctx.enter_context(nc.psum_tensor("a_" + name, [128, 512], F32))

        K1 = HALF + 1
        xin = [sb(f"xin{i}", [HALF, 2, WS, S]) for i in range(2)]
        xw = [sb(f"xw{i}", [K1, 2, NW, TOK]) for i in range(2)]
        xsq = [sb(f"xsq{i}", [HALF, 2, NW, TOK]) for i in range(2)]
        centred = sb("centred", [HALF, 2, WS, S])
        mean = sb("mean", [HALF, B, S])
        rstd = sb("rstd", [HALF, B, S])
        wq, wk = (sb(n, [K1, 2, 2, 4, 32]) for n in ("wq", "wk"))
        wv, ws = (sb(n, [K1, 2, S]) for n in ("wv", "ws"))
        qt = [sb(f"qt{i}", [128, 2, 4 * PAIR]) for i in range(2)]
        kd = [sb(f"kd{i}", [128, 2, 8, 4, TOK]) for i in range(2)]
        vd = sb("vd", [128, 2, 4, 2 * DH + 2])
        half_neg = sb("half_neg", [HALF, TOK])
        ident = sb("ident", [128, 128])
        diag = sb("diag", [128, TOK])
        near0, near1, near2 = (sb(n, [128, TOK + 8]) for n in ("near0", "near1", "near2"))
        best = sb("best", [128, 8])
        ninth = sb("ninth", [128, 8])
        off = sb("off", [128, TOK])
        sc = sb("sc", [128, HEADS, TOK])
        top = sb("top", [128, HEADS])
        prob = sb("prob", [128, HEADS * TOK])
        probt = sb("probt", [128, 4, PAIR])
        rsum = sb("rsum", [128, 4, 2])
        res = sb("res", [128, S])
        score_b, gram_b, v_b, out_b, turn_b, fin_b = map(bank, ("score", "gram", "v", "out", "turn", "fin"))
        qk_b = [bank("qk0"), bank("qk1")]
        OW = 4 * (2 * DH + 2)
        out_o = out_b[:, 0:OW].rearrange("p (a c) -> p a c", a=4)
        out_s = out_b[:, OW:OW + S]

        w_zero, w_in, w_ones = sem("w_zero"), sem("w_in"), sem("w_ones")
        with nc.Block() as block:
            @block.gpsimd
            def _(pool):
                for i in range(2):
                    pool.memset(kd[i][:, :, :, :, :], 0.0)
                pool.memset(ident[:, :], 0.0)
                pool.memset(diag[:, :], 0.0).then_inc(w_ones, 1)
                pool.wait_ge(w_ones, 1)
                pool.affine_select(out=ident[:, :], in_=ident[:, :], compare_op=ALU.not_equal, fill=1.0,
                                   base=0, pattern=[[-1, 128]], channel_multiplier=1).then_inc(w_ones, 1)
                pool.affine_select(out=diag[:, :], in_=diag[:, :], compare_op=ALU.not_equal, fill=FAR,
                                   base=0, pattern=[[-1, TOK]], channel_multiplier=1).then_inc(w_ones, 1)
                pool.wait_ge(w_ones, 3)
                pool.affine_select(out=diag[:, :], in_=diag[:, :], compare_op=ALU.not_equal, fill=FAR,
                                   base=-TOK, pattern=[[-1, TOK]], channel_multiplier=1)

            @block.vector
            def _(dve):
                dve.memset(wq[:, :, :, :, :], 0.0)
                dve.memset(wk[:, :, :, :, :], 0.0).then_inc(w_zero, 1)
                dve.memset(near0[:, TOK:], GUARD)
                dve.memset(ninth[:, :], GUARD)
                dve.memset(half_neg[:, :], -0.5)
                for i in range(2):
                    dve.memset(xw[i][HALF:K1, :, :, :], 1.0)
                for e in range(2):
                    mine, other = slice(e * TOK, (e + 1) * TOK), slice((1 - e) * TOK, (2 - e) * TOK)
                    dve.memset(vd[other, :, :, e * DH:(e + 1) * DH], 0.0)
                    dve.memset(vd[mine, :, :, 2 * DH + e:2 * DH + e + 1], 1.0)
                    dve.memset(vd[other, :, :, 2 * DH + e:2 * DH + e + 1], 0.0)

            @block.sync
            def _(sp):
                sp.wait_ge(w_zero, 1)
                n = 0
                for w, W, b in ((wq, Wq, bq), (wk, Wk, bk)):
                    for a in range(2):
                        sp.dma_start(w[0:HALF, a].rearrange("p m i d -> p (m i) d")[:, :, 0:DH],
                                     W[a * HALF:(a + 1) * HALF, :].rearrange("p (h d) -> p h d", d=DH)).then_inc(w_in, 16)
                    sp.dma_start(w[HALF:K1, 1].rearrange("p m i d -> p (m i) d")[:, :, 0:DH],
                                 b.rearrange("(o h d) -> o h d", o=1, d=DH)).then_inc(w_in, 16)
                    n += 48
                for w, W, b in ((wv, Wv, bv), (ws, Ws, bs)):
                    sp.dma_start(w[0:HALF, :, :], W.rearrange("(a p) n -> p a n", a=2)).then_inc(w_in, 16)
                    sp.dma_start(w[HALF:K1, 1, :], b.rearrange("(o n) -> o n", o=1)).then_inc(w_in, 16)
                    n += 32
                for b in range(B):
                    for t, s in ((mean, 0), (rstd, 1)):
                        sp.dma_start(t[:, b, :], stats[b, s:s + 1, :].broadcast_to([HALF, S])).then_inc(w_in, 16)
                        n += 16
                sp.wait_ge(w_in, n)

        x_in = [sem(f"x_in{i}") for i in range(2)]
        x_out = [sem(f"x_out{i}") for i in range(2)]
        (ready, centred_done, xw_done, sq_done, qk_done, qk_taken, gram_done, picked, score_done, sc_done, exp_done,
         turned, turn_taken, v_ready, v_taken, pv_done, norm_done, fin_done, added) = map(sem, (
             "ready", "centred_done", "xw_done", "sq_done", "qk_done", "qk_taken", "gram_done", "picked", "score_done",
             "sc_done", "exp_done", "turned", "turn_taken", "v_ready", "v_taken", "pv_done", "norm_done", "fin_done",
             "added"))
        THIRDS = PAIRS // 3
        measured = sem("measured")
        sp_waited = sem("sp_waited")
        best_found, best_cut, ninth_found, ninth_cut, off_done, top_done, masked, inverted, weighed = map(sem, (
            "best_found", "best_cut", "ninth_found", "ninth_cut", "off_done", "top_done", "masked", "inverted", "weighed"))
        BODY = 2 * PAIRS
        LOOPS = STRIPS // 2
        xv = x.rearrange("(a p) s n -> p a s n", a=2)
        x1v = x1.rearrange("b (a p) (s n) -> b p a s n", a=2, s=NW)

        def strip(v, s):
            return v[:, :, bass.ds(s, 1), :].rearrange("p a o n -> p a (o n)")

        def flat(t):
            return t[:, :, :, :].rearrange("p a h w -> p a (h w)")

        with nc.Block() as block:
            @block.sync
            def _(sp):
                sp.sem_inc(ready, 1)
                for i in range(2):
                    sp.dma_start(flat(xin[i]), strip(xv, i)).then_inc(x_in[i], 16)

                def two(b, j, last):
                    it = j + b * (NW // 2)
                    for i in range(2):
                        s = 2 * it + i
                        src = None if last else strip(xv, sp.snap(s + 2))
                        dst = strip(x1v[b], 2 * j + i if last else sp.snap(2 * j + i))
                        sp.wait_ge(ready, 1)
                        sp.wait_ge(added, (s + 1) * PAIRS + 1)
                        sp.dma_start(dst, flat(xin[i])).then_inc(x_out[i], 16)
                        if not last:
                            sp.wait_ge(measured, (s + 1) * THIRDS)
                            sp.sem_inc(sp_waited, 1)
                            sp.wait_ge(x_out[i], it * 16 + 16)
                            sp.sem_inc(sp_waited, 1)
                            sp.dma_start(flat(xin[i]), src).then_inc(x_in[i], 16)

                for b in range(B):
                    with sp.Fori(0, NW // 2 - b) as j:
                        two(b, j, False)
                two(B - 1, NW // 2 - 1, True)
                for i in range(2):
                    sp.wait_ge(x_out[i], LOOPS * 16)

            @block.gpsimd
            def _(pool):
                pool.sem_inc(pv_done, 2 * PAIRS)
                pool.sem_inc(xw_done, 1)
                for b in range(B):
                    with pool.Fori(0, NW // 2) as j:
                        for i in range(2):
                            s = (j + b * (NW // 2)) * 2 + i
                            pool.wait_ge(x_in[i], (j + b * (NW // 2)) * 16 + 16)
                            pool.wait_ge(xw_done, s + 1)
                            pool.tensor_tensor(centred[:, :, :, :].rearrange("p a h w -> p (a h) w"),
                                               xin[i][:, :, :, :].rearrange("p a h w -> p (a h) w"),
                                               mean[:, b:b + 1, :].broadcast_to([HALF, 2 * WS, S]),
                                               ALU.subtract).then_inc(centred_done, 1)
                            pool.wait_ge(centred_done, s + 1)
                            pool.wait_ge(pv_done, (s + 1) * PAIRS)
                            for a in range(2):
                                m = pool.tensor_tensor(
                                    xw[i][0:HALF, a].rearrange("p n (h w) -> p n h w", w=WS),
                                    centred[:, a].rearrange("p h (n w) -> p n h w", w=WS),
                                    rstd[:, b, :].rearrange("p (n o w) -> p n o w", o=1, w=WS)
                                    .broadcast_to([HALF, NW, WS, WS]), ALU.mult)
                            m.then_inc(xw_done, 1)
                            pool.wait_ge(xw_done, s + 2)
                            pool.tensor_tensor(xsq[i][:, :, :, :], xw[i][0:HALF], xw[i][0:HALF], ALU.mult).then_inc(sq_done, 1)

            def flow(eng, step):
                step(0, 0, False, None)
                with eng.Fori(0, LOOPS - 1) as it:
                    for p in range(1, BODY):
                        step(it, p, False, (it, p - 1))
                    step(it + 1, 0, False, (it, BODY - 1))
                for p in range(1, BODY):
                    step(LOOPS - 1, p, True, (LOOPS - 1, p - 1))

            def ahead(it, p, by, last):
                if last and p + by >= BODY:
                    return None
                return (it, p + by) if p + by < BODY else (it + 1, p + by - BODY)

            def piece(it, p, last):
                quad = ahead(it, p - p % 4, 4 if p % 4 < 3 else 8, last)
                return quad and (*quad, (p + 1) % 4)

            @block.tensor
            def _(pe):
                def queries_keys(it, p, c):
                    i, quad = p // PAIRS, p // 4
                    Q = it * (BODY // 4) + quad
                    w, m = ((wq, 0), (wq, 1), (wk, 0), (wk, 1))[c]
                    if p % PAIRS == 0 and c == 0:
                        pe.wait_ge(sq_done, it * 2 + i + 1)
                    if c >= 2 or not (isinstance(Q, int) and Q == 0):
                        pe.wait_ge(qk_taken, Q * 4 + c - 1)
                    for a, rows in ((0, HALF), (1, K1)):
                        mm = pe.matmul(qk_b[c % 2][:, :], w[0:rows, a, m].rearrange("p i d -> p (i d)"),
                                       xw[i][0:rows, a, (quad % QUADS) * 8:(quad % QUADS) * 8 + 8, :]
                                       .rearrange("p n t -> p (n t)"), start=a == 0, stop=a == 1)
                    mm.then_inc(qk_done, 1)

                def gram(it, p):
                    i, g = p // PAIRS, it * BODY + p
                    if not (isinstance(g, int) and g == 0):
                        pe.wait_ge(picked, g)
                    for w in range(2):
                        n = 2 * (p % PAIRS) + w
                        o = gram_b[w * TOK:(w + 1) * TOK, 0:TOK]
                        for a in range(2):
                            pe.matmul(o, xw[i][0:HALF, a, n, :], xw[i][0:HALF, a, n, :], start=a == 0, stop=False)
                        for a in range(2):
                            mm = pe.matmul(o, half_neg[:, :], xsq[i][:, a, n, :], start=False, stop=a == 1)
                    mm.then_inc(gram_done, 1)

                def scores(it, p):
                    g = it * BODY + p
                    if p % 4 == 0:
                        pe.wait_ge(qk_taken, (it * (BODY // 4) + p // 4 + 1) * 4)
                    if not (isinstance(g, int) and g == 0):
                        pe.wait_ge(masked, g)
                    for w in range(2):
                        n = 2 * (p % 4) + w
                        for m in range(2):
                            mm = pe.matmul(score_b[w * TOK:(w + 1) * TOK, m * 256:(m + 1) * 256],
                                           qt[p // 4 % 2][:, m, n * TOK:(n + 1) * TOK],
                                           kd[p // 4 % 2][:, m, n].rearrange("p i t -> p (i t)"), start=True, stop=True)
                    mm.then_inc(score_done, 1)

                def values(it, p):
                    i, g = p // PAIRS, it * BODY + p
                    if not (isinstance(g, int) and g == 0):
                        pe.wait_ge(v_taken, g)
                    for w in range(2):
                        n = 2 * (p % PAIRS) + w
                        for e in range(2):
                            for a, rows in ((0, HALF), (1, K1)):
                                mm = pe.matmul(v_b[e * TOK:(e + 1) * TOK, w * HALF:(w + 1) * HALF], xw[i][0:rows, a, n, :],
                                               wv[0:rows, a, :].rearrange("p (h e d) -> p e h d", e=2, d=DH)[:, e],
                                               start=a == 0, stop=a == 1)
                    mm.then_inc(v_ready, 1)

                def turn(it, p):
                    pe.wait_ge(exp_done, it * BODY + p + 1)
                    for a in range(4):
                        mm = pe.transpose(turn_b[:, a * 128:(a + 1) * 128], prob[:, a * 128:(a + 1) * 128], ident[:, :])
                    mm.then_inc(turned, 1)

                def weigh(it, p):
                    i, g = p // PAIRS, it * BODY + p
                    pe.wait_ge(turn_taken, g + 1)
                    pe.wait_ge(v_taken, g + 1)
                    pe.wait_ge(norm_done, g + 1)
                    for w in range(2):
                        for a in range(4):
                            pe.matmul(out_o[w * TOK:(w + 1) * TOK, a, :], probt[:, a, w * TOK:(w + 1) * TOK],
                                      vd[:, w, a, :], start=True, stop=True)
                    n = 2 * (p % PAIRS)
                    for a, rows in ((0, HALF), (1, K1)):
                        mm = pe.matmul(out_s, xw[i][0:rows, a, n:n + 2, :].rearrange("p n t -> p (n t)"),
                                       ws[0:rows, a, :], start=a == 0, stop=a == 1)
                    mm.then_inc(pv_done, 1)

                def back(it, p):
                    g = it * BODY + p
                    pe.wait_ge(norm_done, g + 2)
                    pe.wait_ge(added, g + 1)
                    for a in range(2):
                        mm = pe.transpose(fin_b[0:HALF, a * 128:(a + 1) * 128], res[:, a * HALF:(a + 1) * HALF], ident[:, :])
                    mm.then_inc(fin_done, 1)

                pe.wait_ge(ready, 1)
                for c in range(4):
                    queries_keys(0, 0, c)
                queries_keys(0, 4, 0)
                gram(0, 0)
                scores(0, 0)
                gram(0, 1)
                values(0, 0)

                def step(it, p, last, before):
                    one, two, product = ahead(it, p, 1, last), ahead(it, p, 2, last), piece(it, p, last)
                    if one:
                        scores(*one)
                    turn(it, p)
                    if two:
                        gram(*two)
                    if before:
                        back(*before)
                    if product:
                        queries_keys(*product)
                    weigh(it, p)
                    if one:
                        values(*one)

                flow(pe, step)
                back(LOOPS - 1, BODY - 1)

            @block.scalar
            def _(act):
                def take_qk(it, p, c):
                    quad = p // 4
                    m = c % 2
                    act.wait_ge(qk_done, (it * (BODY // 4) + quad) * 4 + c + 1)
                    if c < 2:
                        act.activation(qt[quad % 2][:, m, :], qk_b[m][:, :], ACT.Copy).then_inc(qk_taken, 1)
                        return
                    for h in range(4):
                        rows = slice(32 * h, 32 * h + 32)
                        e = act.activation(kd[quad % 2][rows, m, :, h, :],
                                           qk_b[m][rows, :].rearrange("p (n t) -> p n t", t=TOK), ACT.Copy)
                    e.then_inc(qk_taken, 1)

                def exps(it, p):
                    g = it * BODY + p
                    act.wait_ge(sc_done, g + 1)
                    act.activation(prob[:, :], sc[:, :, :].rearrange("p h t -> p (h t)"), ACT.Exp,
                                   scale=float(DH) ** -0.5).then_inc(exp_done, 1)

                act.wait_ge(ready, 1)
                for c in range(4):
                    take_qk(0, 0, c)
                take_qk(0, 4, 0)
                exps(0, 0)

                def step(it, p, last, before):
                    g = it * BODY + p
                    one, product = ahead(it, p, 1, last), piece(it, p, last)
                    act.wait_ge(turned, g + 1)
                    act.wait_ge(pv_done, g + 2 * PAIRS)
                    act.activation(probt[:, :, :].rearrange("p a t -> p (a t)"), turn_b[:, :], ACT.Copy).then_inc(turn_taken, 1)
                    if product:
                        take_qk(*product)
                    if one:
                        exps(*one)

                flow(act, step)

            @block.vector
            def _(dve):
                def alone(s, value):
                    dve.wait_ge(ready, 1)
                    dve.wait_ge(s, value)


                def near_in(it, p):
                    g = it * BODY + p
                    dve.wait_ge(gram_done, g + 1)
                    dve.tensor_tensor(near0[:, 0:TOK], gram_b[:, 0:TOK], diag[:, :], ALU.add).then_inc(picked, 1)

                def best_eight(it, p):
                    alone(picked, it * BODY + p + 1)
                    dve.max(best[:, :], near0[:, 0:TOK]).then_inc(best_found, 1)

                def cut_eight(it, p):
                    alone(best_found, it * BODY + p + 1)
                    dve.match_replace(near1[:, :], best[:, :], near0[:, :], TAKEN).then_inc(best_cut, 1)

                def find_ninth(it, p):
                    dve.wait_ge(best_cut, it * BODY + p + 1)
                    dve.tensor_reduce(ninth[:, 0:1], near1[:, 0:TOK], AX.X, ALU.max).then_inc(ninth_found, 1)

                def cut_ninth(it, p):
                    alone(ninth_found, it * BODY + p + 1)
                    dve.match_replace(near2[:, :], ninth[:, :], near1[:, :], TAKEN).then_inc(ninth_cut, 1)

                def offs(it, p):
                    dve.wait_ge(ninth_cut, it * BODY + p + 1)
                    dve.tensor_scalar(off[:, :], near2[:, 0:TOK], 0.5 * (GUARD + TAKEN), OFF, ALU.is_gt, ALU.mult).then_inc(off_done, 1)

                def mask(it, p):
                    g = it * BODY + p
                    dve.wait_ge(score_done, g + 1)
                    dve.wait_ge(off_done, g + 1)
                    if not (isinstance(g, int) and g == 0):
                        dve.wait_ge(exp_done, g)
                    dve.tensor_tensor(sc[:, :, :], score_b[:, :].rearrange("p (h t) -> p h t", t=TOK),
                                      off[:, :].rearrange("p (o t) -> p o t", o=1).broadcast_to([128, HEADS, TOK]),
                                      ALU.add).then_inc(masked, 1)

                def tops(it, p):
                    dve.wait_ge(masked, it * BODY + p + 1)
                    dve.tensor_reduce(top[:, :], sc[:, :, :], AX.X, ALU.max).then_inc(top_done, 1)

                def shift(it, p):
                    dve.wait_ge(top_done, it * BODY + p + 1)
                    dve.tensor_tensor(sc[:, :, :], sc[:, :, :],
                                      top[:, :].rearrange("p (h o) -> p h o", o=1).broadcast_to([128, HEADS, TOK]),
                                      ALU.subtract).then_inc(sc_done, 1)

                def take_v(it, p):
                    dve.wait_ge(v_ready, it * BODY + p + 1)
                    for e in range(2):
                        rows = slice(e * TOK, (e + 1) * TOK)
                        t = dve.tensor_copy(vd[rows, :, :, e * DH:(e + 1) * DH].rearrange("p w a d -> p (w a) d"),
                                            v_b[rows, 0:S].rearrange("p (n d) -> p n d", d=DH))
                    t.then_inc(v_taken, 1)

                def invert(it, p):
                    dve.wait_ge(pv_done, it * BODY + p + 1 + 2 * PAIRS)
                    dve.reciprocal(rsum[:, :, :], out_o[:, :, 2 * DH:]).then_inc(inverted, 1)

                def divide(it, p):
                    dve.wait_ge(inverted, it * BODY + p + 1)
                    dve.tensor_tensor(res[:, :].rearrange("p (a e d) -> p a e d", a=4, e=2),
                                      out_o[:, :, 0:2 * DH].rearrange("p a (e d) -> p a e d", e=2),
                                      rsum[:, :, :].rearrange("p a (e o) -> p a e o", o=1).broadcast_to([128, 4, 2, DH]),
                                      ALU.mult).then_inc(weighed, 1)

                def skip(it, p):
                    dve.wait_ge(weighed, it * BODY + p + 1)
                    dve.tensor_tensor(res[:, :], out_s, res[:, :], ALU.add).then_inc(norm_done, 1)

                def add_up(it, p, a):
                    i = p // PAIRS
                    dve.wait_ge(fin_done, it * BODY + p + 1)
                    c = 2 * WS * (p % PAIRS)
                    v = xin[i][:, a, :, c:c + 2 * WS].rearrange("p h (n w) -> p n h w", w=WS)
                    r = dve.tensor_tensor(v, fin_b[0:HALF, a * 128:(a + 1) * 128]
                                          .rearrange("p (n h w) -> p n h w", n=2, w=WS), v, ALU.add)
                    if a:
                        r.then_inc(added, 1)

                def measure(it, p):
                    i, third = p // PAIRS, p % PAIRS // 3
                    s = it * 2 + i
                    dve.wait_ge(added, it * BODY + p + 2)
                    for g in range(third * (GROUPS // THIRDS), (third + 1) * (GROUPS // THIRDS)):
                        m = dve.bn_stats(st[:, g, bass.ds(s, 1), :].rearrange("p o s -> p (o s)"),
                                         xin[i][:, :, :, g * GW:(g + 1) * GW].rearrange("p a h w -> p (a h) w"))
                    m.then_inc(measured, 1)

                dve.wait_ge(ready, 1)
                dve.sem_inc(norm_done, 1)
                dve.sem_inc(added, 1)
                for stage in (near_in, best_eight, cut_eight, find_ninth, cut_ninth, offs, mask, tops, shift):
                    stage(0, 0)

                def step(it, p, last, before):
                    one = ahead(it, p, 1, last)
                    if one:
                        near_in(*one)
                    if before:
                        invert(*before)
                    if one:
                        best_eight(*one)
                    if before:
                        divide(*before)
                    if one:
                        cut_eight(*one)
                    if before:
                        skip(*before)
                    if one:
                        find_ninth(*one)
                    take_v(it, p)
                    if one:
                        cut_ninth(*one)
                    if one:
                        offs(*one)
                        mask(*one)
                    if before:
                        add_up(*before, 0)
                    if one:
                        tops(*one)
                    if before:
                        add_up(*before, 1)
                    if one:
                        shift(*one)
                    if before and before[1] % 3 == 2:
                        measure(*before)

                flow(dve, step)
                invert(LOOPS - 1, BODY - 1)
                divide(LOOPS - 1, BODY - 1)
                skip(LOOPS - 1, BODY - 1)
                for a in range(2):
                    add_up(LOOPS - 1, BODY - 1, a)
                measure(LOOPS - 1, BODY - 1)


def project_phase(nc, x1, stats, w_in_t, xf, z):
    CH = 4
    with ExitStack() as ctx:
        def sb(name, shape, dt=F32):
            return ctx.enter_context(nc.sbuf_tensor("p_" + name, shape, dt))

        def sem(name):
            return ctx.enter_context(nc.semaphore("p_" + name))

        def bank(name):
            return ctx.enter_context(nc.psum_tensor("p_" + name, [128, 512], F32))

        xt = [sb(f"xt{i}", [HALF, 2 * CH, S]) for i in range(2)]
        xn = [sb(f"xn{i}", [HALF, 2, LINE]) for i in range(2)]
        xo = [sb(f"xo{i}", [128, NJ, CH * S]) for i in range(2)]
        w = sb("w", [HALF, 2, 2 * S])
        gn = sb("gn", [HALF, B, 2, 2])
        ident = sb("ident", [128, 128])
        zero = sb("zero", [128, S])
        turn_b = [bank("turn0"), bank("turn1")]
        out_b = [bank(f"out{m}") for m in range(2 * NJ)]
        w_zero, w_in, w_pad, w_set = sem("w_zero"), sem("w_in"), sem("w_pad"), sem("w_set")
        x_in = [sem(f"x_in{i}") for i in range(2)]
        o_out = [sem(f"o_out{i}") for i in range(2)]
        turned, normed, multiplied, taken_v, taken_a, xo_free = map(
            sem, ("turned", "normed", "multiplied", "taken_v", "taken_a", "xo_free"))
        UNITS = S // CH
        xv = x1.rearrange("b (t l) (f p c) -> b p t (l f) c", l=CH, f=2, c=S)
        STEPS = B * UNITS * 2

        with nc.Block() as block:
            @block.gpsimd
            def _(pool):
                pool.memset(ident[:, :], 0.0).then_inc(w_set, 1)
                pool.wait_ge(w_set, 1)
                pool.affine_select(out=ident[:, :], in_=ident[:, :], compare_op=ALU.not_equal, fill=1.0,
                                   base=0, pattern=[[-1, 128]], channel_multiplier=1)
                pool.memset(zero[:, :], 0.0).then_inc(w_zero, 1)

            @block.sync
            def _(sp):
                sp.dma_start(w[:, :, :], w_in_t.rearrange("(a p) n -> p a n", a=2)).then_inc(w_in, 16)
                n = 16
                with nc.allow_non_contiguous_dma("one column of the statistics"):
                    for b in range(B):
                        for s in range(2):
                            sp.dma_start(gn[:, b, s, :], stats[b, s, :].rearrange("(a p) -> p a", a=2)).then_inc(w_in, 16)
                            n += 16
                sp.wait_ge(w_zero, 1)
                for lo, hi in ((0, 128), (128, S)):
                    for row in (0, S + 1):
                        for b in range(B):
                            sp.dma_start(xf[lo:hi, b, row, :], zero[0:hi - lo, :]).then_inc(w_pad, 16)
                sp.wait_ge(w_in, n)
                sp.wait_ge(w_pad, 16 * 4 * B)

        with nc.Block() as block:
            @block.sync
            def _(sp):
                for b in range(B):
                    with sp.Fori(0, UNITS // 2) as t:
                        for i in range(2):
                            src = xv[b, :, bass.ds(sp.snap(2 * t + i), 1), :, :].rearrange("p o k c -> p (o k) c")
                            u = (t + b * (UNITS // 2)) * 2 + i
                            sp.wait_ge(w_in, 16)
                            sp.wait_ge(turned, u * 2 + 2)
                            sp.dma_start(xt[i][:, :, :], src).then_inc(x_in[i], 16)

            @block.gpsimd
            def _(pool):
                pool.sem_inc(xo_free, 2)
                for b in range(B):
                    with pool.Fori(0, UNITS // 2) as t:
                        for i in range(2):
                            u = (t + b * (UNITS // 2)) * 2 + i
                            first = t * (2 * CH) + i * CH
                            pool.wait_ge(taken_a, u * 2 + 4)
                            pool.wait_ge(taken_v, u * 2 + 4)
                            rows = xf[:, b, bass.ds(first + 1, CH), :].rearrange("d r w -> d (r w)")
                            zs = z[:, b, bass.ds(first * S, CH * S)]
                            for dst, src in ((rows[0:128], xo[i][:, 0, :]), (rows[128:S], xo[i][0:DD, 1, :]),
                                             (zs[0:DD], xo[i][DD:128, 1, :]), (zs[DD:S], xo[i][:, 2, :])):
                                pool.dma_start(dst, src).then_inc(o_out[i], 16)
                            pool.wait_ge(o_out[i], (t + b * (UNITS // 2)) * 64 + 64)
                            pool.sem_inc(xo_free, 1)

            def flow(eng, body):
                for b in range(B):
                    with eng.Fori(0, UNITS // 2 - 1) as t:
                        body(b, t, (b, t + 1))
                    body(b, UNITS // 2 - 1, (b + 1, 0) if b < B - 1 else None)

            def step(b, t, e):
                return (t + b * (UNITS // 2)) * 4 + e

            @block.tensor
            def _(pe):
                pe.sem_inc(turned, 4)
                pe.sem_inc(multiplied, 1)

                def turn(b, t, e):
                    s = step(b, t, e)
                    if e % 2 == 0:
                        pe.wait_ge(x_in[e // 2], (t + b * (UNITS // 2)) * 16 + 16)
                    if not (isinstance(s, int) and s == 0):
                        pe.wait_ge(normed, s)
                    for a in range(2):
                        for k in range(4):
                            mm = pe.transpose(turn_b[a][0:HALF, k * HALF:(k + 1) * HALF],
                                              xt[e // 2][:, (e % 2) * 4 + k, a * HALF:(a + 1) * HALF], ident[0:HALF, 0:HALF])
                    mm.then_inc(turned, 1)

                def multiply(b, t, e):
                    s = step(b, t, e)
                    pe.wait_ge(normed, s + 1)
                    pe.wait_ge(taken_a, s + 1)
                    pe.wait_ge(taken_v, s + 1)
                    for m in range(NJ):
                        for a in range(2):
                            mm = pe.matmul(out_b[(e % 2) * NJ + m][:, 0:LINE], w[:, a, m * 128:(m + 1) * 128],
                                           xn[e % 2][:, a, :], start=a == 0, stop=a == 1)
                    mm.then_inc(multiplied, 1)

                turn(0, 0, 0)

                def body(b, t, after):
                    for e in range(4):
                        if e < 3:
                            turn(b, t, e + 1)
                        elif after:
                            turn(*after, 0)
                        multiply(b, t, e)

                flow(pe, body)

            @block.vector
            def _(dve):
                dve.sem_inc(taken_v, 2)

                def norm(b, t, e):
                    s = step(b, t, e)
                    dve.wait_ge(turned, s + 5)
                    dve.wait_ge(multiplied, s)
                    for a in range(2):
                        m = dve.tensor_scalar(xn[e % 2][:, a, :], turn_b[a][0:HALF, 0:LINE], gn[:, b, 0, a:a + 1],
                                              gn[:, b, 1, a:a + 1], ALU.subtract, ALU.mult)
                    m.then_inc(normed, 1)

                norm(0, 0, 0)

                def body(b, t, after):
                    for e in range(4):
                        if e < 3:
                            norm(b, t, e + 1)
                        elif after:
                            norm(*after, 0)
                        s = step(b, t, e)
                        dve.wait_ge(multiplied, s + 2)
                        if e % 2 == 0:
                            dve.wait_ge(xo_free, (t + b * (UNITS // 2)) * 2 + e // 2 + 1)
                        cols = slice((e % 2) * LINE, (e % 2 + 1) * LINE)
                        dve.tensor_copy(xo[e // 2][:, 0, cols], out_b[(e % 2) * NJ][:, 0:LINE])
                        dve.tensor_copy(xo[e // 2][0:DD, 1, cols], out_b[(e % 2) * NJ + 1][0:DD, 0:LINE]).then_inc(taken_v, 1)

                flow(dve, body)

            @block.scalar
            def _(act):
                act.sem_inc(taken_a, 2)

                def body(b, t, after):
                    for e in range(4):
                        s = step(b, t, e)
                        act.wait_ge(multiplied, s + 2)
                        if e % 2 == 0:
                            act.wait_ge(xo_free, (t + b * (UNITS // 2)) * 2 + e // 2 + 1)
                        cols = slice((e % 2) * LINE, (e % 2 + 1) * LINE)
                        act.activation(xo[e // 2][DD:128, 1, cols], out_b[(e % 2) * NJ + 1][DD:128, 0:LINE], ACT.Silu)
                        act.activation(xo[e // 2][:, 2, cols], out_b[(e % 2) * NJ + 2][:, 0:LINE], ACT.Silu).then_inc(taken_a, 1)

                flow(act, body)


def conv_phase(nc, xf, conv_w, conv_b, xc):
    TAPS = 9
    PEJ = 1
    with ExitStack() as ctx:
        def sb(name, shape, dt=F32):
            return ctx.enter_context(nc.sbuf_tensor("c_" + name, shape, dt))

        def sem(name):
            return ctx.enter_context(nc.semaphore("c_" + name))

        rows_t = [[sb(f"rows{i}_{j}", [128, WS + 2, S + 2]) for j in range(NJ)] for i in range(2)]
        acc = [[sb(f"acc{i}_{j}", [128, WS, S]) for j in range(PEJ, NJ)] for i in range(2)]
        xo = [sb(f"xo{i}", [128, NJ, NB, BLK]) for i in range(2)]
        wt = sb("wt", [128, NJ, TAPS])
        bt = sb("bt", [128, NJ])
        ident = sb("ident", [128, 128])
        tap = sb("tap", [128, TAPS, 128])
        banks = [ctx.enter_context(nc.psum_tensor(f"c_b{q}", [128, 512], F32)) for q in range(SUBS)]
        w_in, w_set, w_edge = sem("w_in"), sem("w_set"), sem("w_edge")
        r_in = [[sem(f"r_in{i}_{j}") for j in range(NJ)] for i in range(2)]
        o_out = [sem(f"o_out{i}") for i in range(2)]
        sp_waited = sem("sp_waited")
        ready, pe_done, banks_read, acc_link, act_done = map(
            sem, ("ready", "pe_done", "banks_read", "acc_link", "act_done"))
        with nc.Block() as block:
            @block.gpsimd
            def _(pool):
                pool.memset(ident[:, :], 0.0).then_inc(w_set, 1)
                pool.wait_ge(w_set, 1)
                pool.affine_select(out=ident[:, :], in_=ident[:, :], compare_op=ALU.not_equal, fill=1.0,
                                   base=0, pattern=[[-1, 128]], channel_multiplier=1).then_inc(w_set, 1)

            @block.sync
            def _(sp):
                n = 0
                with nc.allow_non_contiguous_dma("weights, once"):
                    for b in range(B):
                        rows = slice(b * DD, (b + 1) * DD)
                        sp.dma_start(wt[rows, :, :], conv_w.rearrange("(j p) t -> p j t", p=DD)).then_inc(w_in, 16)
                        sp.dma_start(bt[rows, :], conv_b.rearrange("(j p) -> p j", p=DD)).then_inc(w_in, 16)
                        n += 32
                sp.wait_ge(w_in, n)

            @block.vector
            def _(dve):
                for i in range(2):
                    for j in range(NJ):
                        for c in (0, S + 1):
                            dve.memset(rows_t[i][j][:, :, c:c + 1], 0.0)
                dve.wait_ge(w_in, 64)
                dve.wait_ge(w_set, 2)
                for t in range(TAPS):
                    dve.tensor_scalar(tap[:, t, :], ident[:, :], wt[:, 0, t:t + 1], None, ALU.mult)

        with nc.Block() as block:
            @block.sync
            def _(sp):
                def load(i, c):
                    for j in range(NJ):
                        for b in range(B):
                            sp.dma_start(rows_t[i][j][b * DD:(b + 1) * DD, :, 1:S + 1],
                                         xf[j * DD:(j + 1) * DD, b, bass.ds(c * WS, WS + 2), :]).then_inc(r_in[i][j], 16)

                sp.sem_inc(ready, 1)
                for i in range(2):
                    sp.sem_inc(o_out[i], 16)
                    load(i, i)

                def two(t, last):
                    for i in range(2):
                        c = 2 * t + i
                        sp.wait_ge(act_done, c + 3)
                        sp.sem_inc(sp_waited, 1)
                        sp.dma_start(xc[:, :, bass.ds(c, 1), :, :].rearrange("p j o b n -> p j (o b n)"),
                                     xo[i][:, :, :, :].rearrange("p j b n -> p j (b n)")).then_inc(o_out[i], 16)
                        if not last:
                            load(i, sp.snap(c + 2))

                with sp.Fori(0, NB // 2 - 1) as t:
                    two(t, False)
                two(NB // 2 - 1, True)
                for i in range(2):
                    sp.wait_ge(o_out[i], (NB // 2 + 1) * 16)

            @block.tensor
            def _(pe):
                pe.wait_ge(ready, 1)
                with pe.Fori(0, NB // 2) as t:
                    for i in range(2):
                        c = 2 * t + i
                        pe.wait_ge(r_in[i][0], t * 32 + 32)
                        pe.wait_ge(banks_read, c + 1)
                        for q in range(SUBS):
                            for k in range(TAPS):
                                mm = pe.matmul(banks[q][:, 0:LINE], tap[:, k, :],
                                               rows_t[i][0][:, 2 * q + k // 3:2 * q + k // 3 + 2, k % 3:k % 3 + S],
                                               start=k == 0, stop=k == TAPS - 1)
                            mm.then_inc(pe_done, 1)

            @block.vector
            def _(dve):
                dve.wait_ge(ready, 1)
                with dve.Fori(0, NB // 2) as t:
                    for i in range(2):
                        c = 2 * t + i
                        dve.wait_ge(act_done, c + 1)
                        for k in range(TAPS):
                            for j in range(PEJ, NJ):
                                if k == 0:
                                    dve.wait_ge(r_in[i][j], t * 32 + 32)
                                a = acc[i][j - PEJ][:, :, :]
                                v = rows_t[i][j][:, k // 3:k // 3 + WS, k % 3:k % 3 + S]
                                if k == 0:
                                    m = dve.tensor_scalar(a, v, wt[:, j, 0:1], None, ALU.mult)
                                else:
                                    dve.wait_ge(acc_link, (c * TAPS + k - 1) * (NJ - PEJ) + j - PEJ + 1)
                                    m = dve.scalar_tensor_tensor(out=a, in0=v, scalar=wt[:, j, k:k + 1], in1=a,
                                                                 op0=ALU.mult, op1=ALU.add)
                                m.then_inc(acc_link, 1)

            @block.scalar
            def _(act):
                act.wait_ge(ready, 1)
                act.sem_inc(act_done, 2)
                act.sem_inc(banks_read, 1)

                def out(i, j):
                    return xo[i][:, j].rearrange("p b (h w) -> p h b w", w=WS)

                with act.Fori(0, NB // 2) as t:
                    for i in range(2):
                        c = 2 * t + i
                        act.wait_ge(o_out[i], t * 16 + 16)
                        for q in range(SUBS):
                            act.wait_ge(pe_done, c * SUBS + q + 1)
                            m = act.activation(out(i, 0)[:, 2 * q:2 * q + 2], banks[q][:, 0:LINE]
                                               .rearrange("p (h b w) -> p h b w", h=2, w=WS), ACT.Silu, bias=bt[:, 0:1])
                        m.then_inc(banks_read, 1)
                        for j in range(PEJ, NJ):
                            act.wait_ge(acc_link, ((c + 1) * TAPS - 1) * (NJ - PEJ) + j - PEJ + 1)
                            m = act.activation(out(i, j), acc[i][j - PEJ][:, :, :].rearrange("p h (b w) -> p h b w", w=WS),
                                               ACT.Silu, bias=bt[:, j:j + 1])
                        m.then_inc(act_done, 1)


def final_phase(nc, ysum, z, x1, ln_w, ln_b, w_out_t, out):
    with ExitStack() as ctx:
        def sb(name, shape, dt=F32):
            return ctx.enter_context(nc.sbuf_tensor("f_" + name, shape, dt))

        def sem(name):
            return ctx.enter_context(nc.semaphore("f_" + name))

        def bank(name):
            return ctx.enter_context(nc.psum_tensor("f_" + name, [128, 512], F32))

        TT = WS * S // 128
        T3 = LINE // 128
        yt = [sb(f"yt{i}", [128, NJ, NB, BLK]) for i in range(2)]
        zt = [sb(f"zt{i}", [128, NJ, WS * S]) for i in range(2)]
        rt = [sb(f"rt{i}", [128, B, TT, S]) for i in range(2)]
        yc = [sb(f"yc{i}", [128, NJ, LINE]) for i in range(2)]
        sq = [sb(f"sq{i}", [128, NJ, LINE]) for i in range(2)]
        sd = [sb(f"sd{i}", [128, LINE]) for i in range(2)]
        gated = [sb(f"gated{i}", [128, NJ, LINE]) for i in range(2)]
        mean_of = sb("mean_of", [128, 128])
        wo = sb("wo", [128, NJ, S])
        lnw = sb("lnw", [128, NJ])
        lnb = sb("lnb", [128, NJ])
        epst = sb("epst", [128, 1])
        mean_b, var_b = bank("mean"), bank("var")
        out_b = [[bank(f"out{t}_{b}") for b in range(B)] for t in range(T3)]
        w_in = sem("w_in")
        with nc.Block() as block:
            @block.sync
            def _(sp):
                n = 0
                with nc.allow_non_contiguous_dma("weights, once"):
                    for b in range(B):
                        rows = slice(b * DD, (b + 1) * DD)
                        sp.dma_start(wo[rows, :, :], w_out_t.rearrange("(j p) c -> p j c", p=DD)).then_inc(w_in, 16)
                        sp.dma_start(lnw[rows, :], ln_w.rearrange("(j p) -> p j", p=DD)).then_inc(w_in, 16)
                        sp.dma_start(lnb[rows, :], ln_b.rearrange("(j p) -> p j", p=DD)).then_inc(w_in, 16)
                        n += 48
                sp.wait_ge(w_in, n)

            @block.vector
            def _(dve):
                dve.memset(epst[:, :], LN_EPS)
                for b in range(B):
                    for c in range(B):
                        dve.memset(mean_of[b * DD:(b + 1) * DD, c * DD:(c + 1) * DD], 1.0 / S if b == c else 0.0)

        y_in = [sem(f"y_in{i}") for i in range(2)]
        z_in = [sem(f"z_in{i}") for i in range(2)]
        r_in = [sem(f"r_in{i}") for i in range(2)]
        sp_waited = sem("sp_waited")
        r_out = [sem(f"r_out{i}") for i in range(2)]
        ready, mean_done, yc_done, sq_done, var_done, sd_done, inv_done, scaled, shifted, gated_done, out_done, added = map(
            sem, ("ready", "mean_done", "yc_done", "sq_done", "var_done", "sd_done", "inv_done", "scaled", "shifted",
                  "gated_done", "out_done", "added"))
        LOOPS = NB // 2
        BODY = 2 * SUBS

        def tokens(t, b, c):
            return t[b, bass.ds(c, 1), :].rearrange("o (t p c) -> p (o t) c", p=128, c=S)

        x1v = x1.rearrange("b (c r) n -> b c (r n)", r=WS)
        ov = out.rearrange("b (c r) n -> b c (r n)", r=WS)
        zv = z.rearrange("(j p) b (c n) -> b p j c n", p=DD, n=WS * S)

        with nc.Block() as block:
            @block.sync
            def _(sp):
                def load_y(i, c):
                    sp.dma_start(yt[i][:, :, :, :].rearrange("p j b n -> p j (b n)"),
                                 ysum[:, :, bass.ds(c, 1), :, :].rearrange("p j o b n -> p j (o b n)")).then_inc(y_in[i], 16)

                def load_z(i, c):
                    for b in range(B):
                        sp.dma_start(zt[i][b * DD:(b + 1) * DD, :, :],
                                     zv[b, :, :, bass.ds(c, 1), :].rearrange("p j o n -> p j (o n)")).then_inc(z_in[i], 16)

                def load_r(i, c):
                    for b in range(B):
                        sp.dma_start(rt[i][:, b, :, :], tokens(x1v, b, c)).then_inc(r_in[i], 16)

                def wait(s, v):
                    sp.wait_ge(s, v)
                    sp.sem_inc(sp_waited, 1)

                sp.sem_inc(ready, 1)
                for i in range(2):
                    load_y(i, i)
                    load_z(i, i)
                    load_r(i, i)

                def two(it, last):
                    for i in range(2):
                        steps = (2 * it + i + 1) * SUBS
                        if not last:
                            c = sp.snap(2 * it + i + 2)
                            wait(yc_done, steps)
                            load_y(i, c)
                            wait(gated_done, steps)
                            load_z(i, c)
                        wait(added, steps + 1)
                        for b in range(B):
                            sp.dma_start(tokens(ov, b, 2 * it + i), rt[i][:, b, :, :]).then_inc(r_out[i], 16)
                        if not last:
                            wait(r_out[i], it * (B * 16) + B * 16)
                            load_r(i, c)

                with sp.Fori(0, LOOPS - 1) as it:
                    two(it, False)
                two(LOOPS - 1, True)
                for i in range(2):
                    sp.wait_ge(r_out[i], LOOPS * B * 16)

            def flow(eng, centre, scale, finish):
                centre(0, 0)
                centre(0, 1)
                scale(0, 0)

                def body(it, last):
                    for q in range(BODY):
                        for stage, by in ((centre, 2), (scale, 1), (finish, 0)):
                            if q + by < BODY:
                                stage(it, q + by)
                            elif not last:
                                stage(it + 1, q + by - BODY)

                with eng.Fori(0, LOOPS - 1) as it:
                    body(it, False)
                body(LOOPS - 1, True)

            def nothing(it, q):
                pass

            def lines(i, j, q):
                return yt[i][:, j].rearrange("p b (h w) -> p h b w", w=WS)[:, 2 * (q % SUBS):2 * (q % SUBS) + 2]

            def grid(ap):
                return ap.rearrange("p (h b w) -> p h b w", h=2, w=WS)

            def later(s, by=1):
                return not (isinstance(s, int) and s < by)

            @block.tensor
            def _(pe):
                pe.wait_ge(ready, 1)
                pe.sem_inc(out_done, 2)

                def centre(it, q):
                    s = it * BODY + q
                    if q % SUBS == 0:
                        pe.wait_ge(y_in[q // SUBS], it * 16 + 16)
                    if later(s):
                        pe.wait_ge(yc_done, s)
                    for j in range(NJ):
                        mm = pe.matmul(mean_b[:, 0:LINE], mean_of[:, :], lines(q // SUBS, j, q),
                                       start=j == 0, stop=j == NJ - 1)
                    mm.then_inc(mean_done, 1)

                def scale(it, q):
                    s = it * BODY + q
                    pe.wait_ge(sq_done, s + 1)
                    if later(s):
                        pe.wait_ge(sd_done, s)
                    for j in range(NJ):
                        mm = pe.matmul(var_b[:, 0:LINE], mean_of[:, :], sq[q % 2][:, j, :],
                                       start=j == 0, stop=j == NJ - 1)
                    mm.then_inc(var_done, 1)

                def finish(it, q):
                    s = it * BODY + q
                    pe.wait_ge(gated_done, s + 1)
                    pe.wait_ge(added, s + 1)
                    for t in range(T3):
                        for b in range(B):
                            rows = slice(b * DD, (b + 1) * DD)
                            for j in range(NJ):
                                mm = pe.matmul(out_b[t][b][:, 0:S], gated[q % 2][rows, j, t * 128:(t + 1) * 128],
                                               wo[rows, j, :], start=j == 0, stop=j == NJ - 1)
                    mm.then_inc(out_done, 1)

                flow(pe, centre, scale, finish)

            @block.vector
            def _(dve):
                dve.wait_ge(ready, 1)
                dve.sem_inc(added, 1)

                def centre(it, q):
                    s = it * BODY + q
                    dve.wait_ge(mean_done, s + 1)
                    if later(s, 2):
                        dve.wait_ge(shifted, s - 1)
                    for j in range(NJ):
                        m = dve.tensor_tensor(grid(yc[q % 2][:, j, :]), lines(q // SUBS, j, q),
                                              grid(mean_b[:, 0:LINE]), ALU.subtract)
                    m.then_inc(yc_done, 1)

                def scale(it, q):
                    s = it * BODY + q
                    dve.wait_ge(sd_done, s + 1)
                    dve.reciprocal(sd[q % 2][:, :], sd[q % 2][:, :]).then_inc(inv_done, 1)
                    dve.wait_ge(inv_done, s + 1)
                    dve.tensor_tensor(yc[q % 2][:, :, :], yc[q % 2][:, :, :],
                                      sd[q % 2][:, :].rearrange("p (o t) -> p o t", o=1).broadcast_to([128, NJ, LINE]),
                                      ALU.mult).then_inc(scaled, 1)

                def finish(it, q):
                    i, s = q // SUBS, it * BODY + q
                    if q % SUBS == 0:
                        dve.wait_ge(r_in[i], it * (B * 16) + B * 16)
                    dve.wait_ge(out_done, s + 3)
                    for t in range(T3):
                        for b in range(B):
                            v = rt[i][:, b, T3 * (q % SUBS) + t, :]
                            m = dve.tensor_tensor(v, out_b[t][b][:, 0:S], v, ALU.add)
                    m.then_inc(added, 1)

                flow(dve, centre, scale, finish)

            @block.scalar
            def _(act):
                act.wait_ge(ready, 1)

                def centre(it, q):
                    s = it * BODY + q
                    act.wait_ge(yc_done, s + 1)
                    if later(s, 2):
                        act.wait_ge(gated_done, s - 1)
                    act.activation(sq[q % 2][:, :, :], yc[q % 2][:, :, :], ACT.Square).then_inc(sq_done, 1)

                def scale(it, q):
                    s = it * BODY + q
                    act.wait_ge(var_done, s + 1)
                    act.activation(sd[q % 2][:, :], var_b[:, 0:LINE], ACT.Sqrt, bias=epst[:, 0:1]).then_inc(sd_done, 1)
                    act.wait_ge(scaled, s + 1)
                    for j in range(NJ):
                        m = act.activation(sq[q % 2][:, j, :], yc[q % 2][:, j, :], ACT.Identity,
                                           scale=lnw[:, j:j + 1], bias=lnb[:, j:j + 1])
                    m.then_inc(shifted, 1)

                flow(act, centre, scale, nothing)

            @block.gpsimd
            def _(pool):
                pool.wait_ge(ready, 1)

                def scale(it, q):
                    i, s = q // SUBS, it * BODY + q
                    pool.wait_ge(shifted, s + 1)
                    if q % SUBS == 0:
                        pool.wait_ge(z_in[i], it * (B * 16) + B * 16)
                    if later(s):
                        pool.wait_ge(out_done, s + 1)
                    pool.tensor_tensor(gated[q % 2][:, :, :], sq[q % 2][:, :, :],
                                       zt[i][:, :, (q % SUBS) * LINE:(q % SUBS + 1) * LINE], ALU.mult).then_inc(gated_done, 1)

                flow(pool, nothing, scale, nothing)


def scan_phase(nc, xc, ysum, x_proj_w_t, dt_projs_w_t, dt_projs_b, A_logs, Ds, directions=range(K)):
    with ExitStack() as ctx:
        def sb(name, shape, dt=F32):
            return ctx.enter_context(nc.sbuf_tensor(name, shape, dt))

        def sem(name):
            return ctx.enter_context(nc.semaphore(name))

        u = [sb(f"u{i}", [128, NJ, NB, BLK]) for i in range(2)]
        yt = [sb(f"yt{i}", [128, NJ, NB, BLK]) for i in range(2)]
        decay = [sb(f"decay{i}", [128, NJ, LINE + 1]) for i in range(4)]
        state = [sb(f"state{i}", [128, NJ, LINE + 1]) for i in range(4)]
        prod = [sb(f"prod{i}", [128, NJ, LINE]) for i in range(4)]
        cb = [sb(f"cb{i}", [128, LINE]) for i in range(4)]
        delta = [sb(f"delta{i}", [128, NJ, LINE]) for i in range(2)]
        du = [sb(f"du{i}", [128, NJ, LINE]) for i in range(2)]
        tail = sb("tail", [128, NJ, LINE])
        low = sb("low", [128, NJ, LINE])
        high = sb("high", [128, NJ, LINE])
        ln_one = sb("ln_one", [128, 2])
        consts = sb("consts", [128, 2])
        relu = sb("relu", [128, NJ, LINE])
        bc3 = [sb(f"bc3_{i}", [3 * NBC, LINE], BF16) for i in range(4)]
        rest = sb("rest", [2 * NBC, LINE])
        dts = sb("dts", [XR + 1, LINE])
        carry = sb("carry", [128, N, NJ])
        ident = sb("ident", [128, 128])
        sel = sb("sel", [3 * NBC, 2, N, B, DD], BF16)
        xpw = sb("xpw", [128, K, NJ, XR])
        dtw = sb("dtw", [XR + 1, K, NJ, 128])
        a_neg = sb("a_neg", [128, K * NJ, N])
        a_exp = sb("a_exp", [128, K * NJ, N])
        ds_t = sb("ds_t", [128, K * NJ])
        dsum = sb("dsum", [128, NJ])

        ybank = ctx.enter_context(nc.psum_tensor("ybank", [128, NJ, 512], F32))
        bbank = ctx.enter_context(nc.psum_tensor("bbank", [128, 2, 512], F32))
        cbank = ctx.enter_context(nc.psum_tensor("cbank", [128, 512], F32))
        pbank = ctx.enter_context(nc.psum_tensor("pbank", [128, 2, 512], F32))

        w_zero, w_in, w_set, w_exp, w_one = sem("w_zero"), sem("w_in"), sem("w_set"), sem("w_exp"), sem("w_one")
        n_in = [0]
        with nc.Block() as block:
            @block.gpsimd
            def _(pool):
                pool.memset(ident[:, :], 0.0).then_inc(w_zero, 1)
                pool.memset(sel[:, :, :, :, :], 0.0).then_inc(w_zero, 1)
                pool.memset(xpw[:, :, :, :], 0.0).then_inc(w_zero, 1)
                pool.memset(dtw[:, :, :, :], 0.0).then_inc(w_zero, 1)
                pool.memset(dts[:, :], 1.0).then_inc(w_zero, 1)
                pool.wait_ge(w_zero, 5)
                pool.affine_select(out=ident[:, :], in_=ident[:, :], compare_op=ALU.not_equal, fill=1.0,
                                   base=0, pattern=[[-1, 128]], channel_multiplier=1).then_inc(w_set, 1)
                done = 1
                for part in range(3):
                    for w in range(2):
                        pool.wait_ge(w_set, done)
                        pool.affine_select(out=sel[:, w], in_=sel[:, w], compare_op=ALU.not_equal,
                                           fill=1.0, base=-(NBC * part + B * N * w),
                                           pattern=[[-1, N], [-N, B], [0, DD]],
                                           channel_multiplier=1).then_inc(w_set, 1)
                        done += 1

            @block.sync
            def _(sp):
                sp.wait_ge(w_zero, 5)
                with nc.allow_non_contiguous_dma("weights, once"):
                    for b in range(B):
                        rows = slice(b * DD, (b + 1) * DD)
                        for j in range(NJ):
                            w = x_proj_w_t[j * DD:(j + 1) * DD, :, :]
                            for lo, n, to in ((R, N, b * N), (R + N, N, B * N + b * N), (0, R, NBC + b * R)):
                                sp.dma_start(xpw[rows, :, j, to:to + n], w[:, :, lo:lo + n]).then_inc(w_in, 16)
                                n_in[0] += 16
                        sp.dma_start(dtw[NBC + b * R:NBC + (b + 1) * R, :, :, rows].rearrange("r k j p -> r (k j) p"),
                                     dt_projs_w_t.rearrange("r k (j p) -> r (k j) p", p=DD)).then_inc(w_in, 16)
                        n_in[0] += 16
                        sp.dma_start(dtw[XR:XR + 1, :, :, rows].rearrange("o k j p -> o (k j) p"),
                                     dt_projs_b.rearrange("(o k) (j p) -> o (k j) p", o=1, p=DD)).then_inc(w_in, 16)
                        sp.dma_start(a_exp[rows, :, :],
                                     A_logs.rearrange("k (j p) n -> p (k j) n", p=DD)).then_inc(w_in, 16)
                        sp.dma_start(ds_t[rows, :], Ds.rearrange("k (j p) -> p (k j)", p=DD)).then_inc(w_in, 16)
                        n_in[0] += 48
                sp.wait_ge(w_in, n_in[0])

            @block.scalar
            def _(act):
                act.wait_ge(w_in, n_in[0])
                act.preload_act_table_set("natural_log_exp_and_others")
                act.activation(a_exp[:, :, :], a_exp[:, :, :], ACT.Exp).then_inc(w_exp, 1)
                act.wait_ge(w_one, 1)
                act.activation(ln_one[:, 0:1], ln_one[:, 0:1], ACT.Ln).then_inc(w_exp, 1)

            @block.vector
            def _(dve):
                dve.memset(consts[:, 0:1], -SPLIT)
                dve.memset(consts[:, 1:2], C1 / (2 * C2 ** 0.5))
                dve.memset(ln_one[:, :], 1.0).then_inc(w_one, 1)
                for i in range(4):
                    dve.memset(decay[i][:, :, LINE:], 0.0)
                dve.wait_ge(w_exp, 2)
                dve.tensor_scalar(ln_one[:, 1:2], ln_one[:, 0:1], -1.0, None, ALU.mult)
                dve.tensor_scalar(a_neg[:, :, :], a_exp[:, :, :], -1.0, None, ALU.mult)
                dve.tensor_reduce(dsum[:, :], ds_t[:, :].rearrange("p (k j) -> p j k", j=NJ),
                                  mybir.AxisListType.X, ALU.add)

        def lines(tile, j, col, first):
            if col:
                return tile[:, j].rearrange("p b (h w) -> p w b h", w=WS)[:, first:first + 2]
            return tile[:, j].rearrange("p b (h w) -> p h b w", w=WS)[:, first:first + 2]

        NPAIR = NB // 2
        QS = 2 * SUBS

        START = N - 3
        TAKE = 2

        def ahead(it, q, by, last):
            if last and q + by >= QS:
                return None
            return (it, q + by) if q + by < QS else (it + 1, q + by - QS)

        def later(s):
            return not (isinstance(s, int) and s == 0)

        ready = sem("ready")
        sp_waited = sem("sp_waited")
        u_in = [sem(f"u_in{i}") for i in range(2)]
        y_in = [sem(f"y_in{i}") for i in range(2)]
        y_out = [sem(f"y_out{i}") for i in range(2)]
        xp_done, dt_ready, bc_hi, bc_rest, bc_mid, bc_ready = map(
            sem, ("xp_done", "dt_ready", "bc_hi", "bc_rest", "bc_mid", "bc_ready"))
        dt_done, dt_taken, soft_ready, delta_ready, du_ready = map(
            sem, ("dt_done", "dt_taken", "soft_ready", "delta_ready", "du_ready"))
        high_ready, low_ready, quad_ready, log_low, log_ready = map(
            sem, ("high_ready", "low_ready", "quad_ready", "log_low", "log_ready"))
        b_ready, c_ready, c_copied, decay_ready = map(sem, ("b_ready", "c_ready", "c_copied", "decay_ready"))
        drive_done, scan_done, prod_done, carry_done, acc_done, y_done = map(
            sem, ("drive_done", "scan_done", "prod_done", "carry_done", "acc_done", "y_done"))
        start_done = sem("start_done")

        def direction(block, turn, k):
            col, rev = k % 2 == 1, k >= 2

            def chunk(c):
                return NB - 1 - c if rev else c

            def first_line(q):
                return (WS - 2 - 2 * (q % SUBS)) if rev else 2 * (q % SUBS)

            def at(it, q):
                return (it + turn * NPAIR) * QS + q

            def tiles(it):
                return (it + turn * NPAIR) * 16

            def part(t, c):
                c = bass.ds(c, 1)
                return (t[:, :, :, c, :] if col else t[:, :, c, :, :]).rearrange("p j a b n -> p j (a b) n")

            @block.sync
            def _(sp):
                def wait(s, v):
                    sp.wait_ge(s, v)
                    sp.sem_inc(sp_waited, 1)

                for i in range(2):
                    if turn == 0:
                        sp.sem_inc(y_out[i], 16)
                    sp.dma_start(u[i][:, :, :, :], part(xc, chunk(i))).then_inc(u_in[i], 16)
                if turn:
                    for i in range(2):
                        sp.wait_ge(y_out[i], tiles(1))
                    for i in range(2):
                        sp.dma_start(yt[i][:, :, :, :], part(ysum, chunk(i))).then_inc(y_in[i], 16)

                def chunk_pair(it, last):
                    for i in range(2):
                        here = sp.snap(chunk(2 * it + i)) if not last else chunk(2 * it + i)
                        wait(y_done, at(it, (i + 1) * SUBS) + 1)
                        sp.dma_start(part(ysum, here), yt[i][:, :, :, :]).then_inc(y_out[i], 16)
                        if not last:
                            after = sp.snap(chunk(2 * it + i + 2))
                            sp.dma_start(u[i][:, :, :, :], part(xc, after)).then_inc(u_in[i], 16)
                            if turn:
                                wait(y_out[i], tiles(it + 2))
                                sp.dma_start(yt[i][:, :, :, :], part(ysum, after)).then_inc(y_in[i], 16)

                with sp.Fori(0, NPAIR - 1) as it:
                    chunk_pair(it, False)
                chunk_pair(NPAIR - 1, True)
                if turn == len(directions) - 1:
                    for i in range(2):
                        sp.wait_ge(y_out[i], tiles(NPAIR + 1))

            def pairs(eng, step):
                step(0, 0, False, None)
                with eng.Fori(0, NPAIR - 1) as it:
                    for q in range(1, QS):
                        step(it, q, False, (it, q - 1))
                    step(it + 1, 0, False, (it, QS - 1))
                for q in range(1, QS):
                    step(NPAIR - 1, q, True, (NPAIR - 1, q - 1))

            @block.tensor
            def _(pe):
                def x_proj(it, q):
                    s = at(it, q)
                    if q % SUBS == 0:
                        pe.wait_ge(u_in[q // SUBS % 2], tiles(it + 1))
                    if later(s):
                        pe.wait_ge(dt_taken, s * NJ)
                    for j in range(NJ):
                        mm = pe.matmul(pbank[0:XR, 0, 0:LINE], xpw[:, k, j, :],
                                       lines(u[q // SUBS % 2], j, col, first_line(q)),
                                       start=j == 0, stop=j == NJ - 1)
                    mm.then_inc(xp_done, 1)

                def step_size(it, q, j):
                    s = at(it, q)
                    if j == 0:
                        pe.wait_ge(dt_ready, s + 1)
                    if j == 1:
                        pe.wait_ge(bc_rest, s + 1)
                    if j == 2 or (j == 0 and later(s)):
                        pe.wait_ge(dt_taken, s * NJ + j // 2)
                    pe.matmul(pbank[:, (j + 1) % 2, 0:LINE], dtw[NBC:XR + 1, k, j, :], dts[NBC:XR + 1, :],
                              start=True, stop=True).then_inc(dt_done, 1)

                def spread_b(it, q, n):
                    if n == 0:
                        pe.wait_ge(bc_ready, at(it, q) + 1)
                    pe.wait_ge(drive_done, at(it, q) * N + n + 1)
                    pe.matmul(bbank[:, n % 2, 0:LINE], sel[:, 0, n].rearrange("r b d -> r (b d)"),
                              bc3[q % 4][:, :], start=True, stop=True).then_inc(b_ready, 1)

                def spread_c(it, q, n):
                    g = at(it, q) * N + n
                    if later(g):
                        pe.wait_ge(c_copied, g)
                    pe.matmul(cbank[:, 0:LINE], sel[:, 1, n].rearrange("r b d -> r (b d)"),
                              bc3[q % 4][:, :], start=True, stop=True).then_inc(c_ready, 1)

                def add_up(it, q, n):
                    pe.wait_ge(prod_done, at(it, q) * N + n + 5)
                    if n == 0:
                        pe.wait_ge(y_done, at(it, q) + 1)
                    for j in range(NJ):
                        mm = pe.matmul(ybank[:, j, 0:LINE], ident[:, :], prod[n % 4][:, j, :],
                                       start=n == 0, stop=n == N - 1)
                    mm.then_inc(acc_done, 1)

                x_proj(0, 0)
                for j in range(NJ):
                    step_size(0, 0, j)
                spread_b(0, 0, 0)
                spread_b(0, 0, 1)
                spread_c(0, 0, 0)
                x_proj(0, 1)
                for j in range(NJ):
                    step_size(0, 1, j)

                def step(it, q, last, before):
                    one, two = ahead(it, q, 1, last), ahead(it, q, 2, last)
                    for n in range(N):
                        if n < N - 2:
                            spread_b(it, q, n + 2)
                        elif one:
                            spread_b(*one, n + 2 - N)
                        if n < N - 1:
                            spread_c(it, q, n + 1)
                        elif one:
                            spread_c(*one, 0)
                        if two and n == 2:
                            x_proj(*two)
                        if two and n >= 4 and n < 4 + NJ:
                            step_size(*two, n - 4)
                        if n >= 2:
                            add_up(it, q, n - 2)
                        elif before:
                            add_up(*before, n + N - 2)

                pairs(pe, step)
                add_up(NPAIR - 1, QS - 1, N - 2)
                add_up(NPAIR - 1, QS - 1, N - 1)

            @block.scalar
            def _(act):
                def front(it, q):
                    act.wait_ge(xp_done, at(it, q) + 1)
                    act.activation(bc3[q % 4][0:NBC, :], pbank[0:NBC, 0, 0:LINE], ACT.Copy).then_inc(bc_hi, 1)
                    act.activation(dts[NBC:XR, :], pbank[NBC:XR, 0, 0:LINE], ACT.Copy).then_inc(dt_ready, 1)

                def middle(it, q):
                    act.wait_ge(bc_rest, at(it, q) + 1)
                    act.activation(bc3[q % 4][NBC:2 * NBC, :], rest[NBC:2 * NBC, :], ACT.Copy).then_inc(bc_mid, 1)

                def take(it, q, j):
                    s = at(it, q)
                    if j == 0 and later(s):
                        act.wait_ge(delta_ready, s)
                    act.wait_ge(dt_done, s * NJ + j + 1)
                    act.activation(tail[:, j, :], pbank[:, (j + 1) % 2, 0:LINE], ACT.Abs)
                    act.activation(relu[:, j, :], pbank[:, (j + 1) % 2, 0:LINE], ACT.Relu).then_inc(dt_taken, 1)

                def soft_exp(it, q):
                    act.wait_ge(dt_taken, (at(it, q) + 1) * NJ)
                    act.activation(tail[:, :, :], tail[:, :, :], ACT.Exp, scale=-1.0).then_inc(soft_ready, 1)

                def soft_high(it, q):
                    act.wait_ge(soft_ready, 2 * at(it, q) + 1)
                    act.activation(high[:, :, :], tail[:, :, :], ACT.Relu, bias=consts[:, 0:1]).then_inc(high_ready, 1)

                def soft_quad(it, q):
                    act.wait_ge(low_ready, at(it, q) + 1)
                    act.wait_ge(high_ready, at(it, q) + 1)
                    act.activation(tail[:, :, :], low[:, :, :], ACT.Square, scale=C2 ** 0.5,
                                   bias=consts[:, 1:2]).then_inc(quad_ready, 1)

                def soft_ln(it, q):
                    act.activation(high[:, :, :], high[:, :, :], ACT.Ln, scale=1.0 / (1.0 + SPLIT),
                                   bias=1.0).then_inc(soft_ready, 1)

                def copy_c(it, q, n):
                    g = at(it, q) * N + n
                    act.wait_ge(c_ready, g + 1)
                    act.wait_ge(prod_done, g + 1)
                    act.activation(cb[n % 4][:, :], cbank[:, 0:LINE], ACT.Copy).then_inc(c_copied, 1)

                def decays(it, q, n):
                    if n == 0:
                        act.wait_ge(delta_ready, at(it, q) + 1)
                    act.wait_ge(scan_done, at(it, q) * N + n + 1)
                    for j in range(NJ):
                        e = act.activation(decay[n % 4][:, j, 0:LINE], delta[q % 2][:, j, :], ACT.Exp,
                                           scale=a_neg[:, k * NJ + j, n:n + 1])
                    e.then_inc(decay_ready, 1)

                def starts(it, q, n):
                    act.wait_ge(carry_done, at(it, q) * N + n + START)
                    act.activation(state[n % 4][:, 0:NJ - 1, LINE], carry[:, n, 0:NJ - 1] if rev else carry[:, n, 1:NJ],
                                   ACT.Copy).then_inc(start_done, 1)

                def start_sums(it, q, j):
                    i = q // SUBS % 2
                    if j == 0:
                        act.wait_ge(u_in[i], tiles(it + 1))
                        act.wait_ge(y_out[i], tiles(it + 1))
                    m = act.activation(yt[i][:, j], u[i][:, j], ACT.Copy, scale=dsum[:, j:j + 1])
                    if j == NJ - 1:
                        m.then_inc(y_in[i], 16)

                if turn == 0:
                    act.preload_act_table_set("natural_log_exp_and_others")
                front(0, 0)
                middle(0, 0)
                for j in range(NJ):
                    take(0, 0, j)
                soft_exp(0, 0)
                soft_high(0, 0)
                soft_quad(0, 0)
                soft_ln(0, 0)
                front(0, 1)
                decays(0, 0, 0)
                decays(0, 0, 1)
                act.wait_ge(ready, turn + 1)
                starts(0, 0, 0)
                middle(0, 1)
                for j in range(NJ):
                    take(0, 1, j)
                soft_exp(0, 1)

                def step(it, q, last, before):
                    one, two = ahead(it, q, 1, last), ahead(it, q, 2, last)
                    for n in range(N):
                        copy_c(it, q, n)
                        if n < N - 2:
                            decays(it, q, n + 2)
                        elif one:
                            decays(*one, n + 2 - N)
                        if n < N - 1:
                            starts(it, q, n + 1)
                        elif one:
                            starts(*one, 0)
                        if one and n == 0:
                            soft_high(*one)
                        if one and n == 1:
                            soft_quad(*one)
                        if one and n == 2:
                            soft_ln(*one)
                        if two and n == 3:
                            front(*two)
                        if two and n >= 5:
                            take(*two, n - 5)
                        if two and n == 5:
                            middle(*two)
                        if two and n == 7:
                            soft_exp(*two)
                        if turn == 0 and q % SUBS == 0 and n >= 2 and n < 2 + NJ:
                            start_sums(it, q, n - 2)

                pairs(act, step)

            @block.gpsimd
            def _(pool):
                if turn == 0:
                    pool.sem_inc(carry_done, N)
                    for s, tiles_of in ((drive_done, 2), (scan_done, 4), (prod_done, 4), (acc_done, 4)):
                        pool.sem_inc(s, tiles_of)
                else:
                    pool.wait_ge(carry_done, at(0, 0) * N + N)
                pool.memset(carry[:, :, :], 0.0).then_inc(ready, 1)

                def deltas(it, q):
                    pool.wait_ge(log_ready, at(it, q) + 1)
                    pool.tensor_tensor(delta[q % 2][:, :, :], relu[:, :, :], low[:, :, :], ALU.add).then_inc(delta_ready, 1)

                def delta_u(it, q):
                    i = q // SUBS % 2
                    if q % SUBS == 0:
                        pool.wait_ge(u_in[i], tiles(it + 1))
                    pool.wait_ge(delta_ready, at(it, q) + 1)
                    for j in range(NJ):
                        v = lines(u[i], j, col, first_line(q))
                        m = pool.tensor_tensor(du[q % 2][:, j, :].rearrange("p (l a b) -> p l a b", l=2, b=WS),
                                               delta[q % 2][:, j, :].rearrange("p (l a b) -> p l a b", l=2, b=WS),
                                               v, ALU.mult)
                    m.then_inc(du_ready, 1)

                deltas(0, 0)
                delta_u(0, 0)
                edge = 0 if rev else LINE - 1

                def step(it, q, last, before):
                    one = ahead(it, q, 1, last)
                    for n in range(N):
                        g = at(it, q) * N + n
                        pool.wait_ge(scan_done, g + 5)
                        pool.wait_ge(c_copied, g + 1)
                        pool.wait_ge(acc_done, g + 1)
                        pool.tensor_tensor(prod[n % 4][:, :, :], state[n % 4][:, :, 0:LINE],
                                           cb[n % 4][:, :].rearrange("p (o t) -> p o t", o=1).broadcast_to([128, NJ, LINE]),
                                           ALU.mult).then_inc(prod_done, 1)
                        pool.tensor_copy(carry[:, n, :], state[n % 4][:, :, edge]).then_inc(carry_done, 1)
                        if one and n == 3:
                            deltas(*one)
                        if one and n == 4:
                            delta_u(*one)

                pairs(pool, step)

            @block.vector
            def _(dve):
                if turn == 0:
                    dve.sem_inc(y_done, 1)

                def split(it, q):
                    dve.wait_ge(bc_hi, at(it, q) + 1)
                    dve.tensor_tensor(rest[NBC:2 * NBC, :], pbank[0:NBC, 0, 0:LINE], bc3[q % 4][0:NBC, :],
                                      ALU.subtract).then_inc(bc_rest, 1)

                def split_low(it, q):
                    dve.wait_ge(bc_mid, at(it, q) + 1)
                    dve.tensor_tensor(bc3[q % 4][2 * NBC:3 * NBC, :], rest[NBC:2 * NBC, :],
                                      bc3[q % 4][NBC:2 * NBC, :], ALU.subtract).then_inc(bc_ready, 1)

                def soft_low(it, q):
                    s = at(it, q)
                    dve.wait_ge(soft_ready, 2 * s + 1)
                    if later(s):
                        dve.wait_ge(delta_ready, s)
                    dve.tensor_scalar(low[:, :, :], tail[:, :, :], SPLIT, None, ALU.min).then_inc(low_ready, 1)

                def soft_log(it, q):
                    dve.wait_ge(quad_ready, at(it, q) + 1)
                    dve.scalar_tensor_tensor(out=low[:, :, :], in0=tail[:, :, :], scalar=C0 - C1 * C1 / (4 * C2),
                                             in1=low[:, :, :], op0=ALU.add, op1=ALU.mult).then_inc(log_low, 1)

                def soft_sum(it, q):
                    s = at(it, q)
                    dve.wait_ge(soft_ready, 2 * s + 2)
                    dve.wait_ge(log_low, s + 1)
                    dve.scalar_tensor_tensor(out=low[:, :, :], in0=high[:, :, :], scalar=ln_one[:, 1:2],
                                             in1=low[:, :, :], op0=ALU.add, op1=ALU.add).then_inc(log_ready, 1)

                def drive_in(it, q, n):
                    g = at(it, q) * N + n
                    if n == 0:
                        dve.wait_ge(du_ready, at(it, q) + 1)
                    dve.wait_ge(b_ready, g + 1)
                    dve.wait_ge(carry_done, g + START)
                    dve.tensor_tensor(state[n % 4][:, :, 0:LINE], du[q % 2][:, :, :],
                                      bbank[:, n % 2:n % 2 + 1, 0:LINE].broadcast_to([128, NJ, LINE]),
                                      ALU.mult).then_inc(drive_done, 1)

                first = NJ - 1 if rev else 0

                def scan(it, q, n):
                    g = at(it, q) * N + n
                    dve.wait_ge(decay_ready, g + 1)
                    dve.wait_ge(drive_done, g + 3)
                    dve.wait_ge(start_done, g + 1)
                    run = slice(0, NJ * (LINE + 1) - 1)
                    a, h = (t[n % 4][:, :, :].rearrange("p j t -> p (j t)")[:, run] for t in (decay, state))
                    if rev:
                        a, h = a[:, ::-1], h[:, ::-1]
                    sc = dve.tensor_tensor_scan(out=h, data0=a, data1=h, initial=carry[:, n, first:first + 1],
                                                op0=ALU.mult, op1=ALU.add)
                    sc.then_inc(scan_done, 1)

                def take_y(it, q):
                    i = q // SUBS % 2
                    if q % SUBS == 0:
                        dve.wait_ge(y_in[i], tiles(it + 1))
                    dve.wait_ge(acc_done, (at(it, q) + 1) * N + 4)
                    for j in range(NJ):
                        v = lines(yt[i], j, col, first_line(q))
                        ad = dve.tensor_tensor(v, ybank[:, j, 0:LINE].rearrange("p (l a b) -> p l a b", l=2, b=WS),
                                               v, ALU.add)
                    ad.then_inc(y_done, 1)

                def step(it, q, last, before):
                    one, two = ahead(it, q, 1, last), ahead(it, q, 2, last)
                    for n in range(N):
                        if n < N - 1:
                            drive_in(it, q, n + 1)
                        elif one:
                            drive_in(*one, 0)
                        if before and n == TAKE:
                            take_y(*before)
                        scan(it, q, n)
                        if one and n == 0:
                            soft_low(*one)
                        if one and n == 3:
                            soft_log(*one)
                            soft_sum(*one)
                        if two and n == 4:
                            split(*two)
                        if two and n == 6:
                            split_low(*two)

                split(0, 0)
                split_low(0, 0)
                soft_low(0, 0)
                soft_log(0, 0)
                soft_sum(0, 0)
                drive_in(0, 0, 0)
                dve.wait_ge(ready, turn + 1)
                split(0, 1)
                split_low(0, 1)
                pairs(dve, step)
                take_y(NPAIR - 1, QS - 1)

        with nc.Block() as block:
            for turn, k in enumerate(directions):
                direction(block, turn, k)


def build(nc, x, Wq, bq, Wk, bk, Wv, bv, Wskip, bskip, in_w_t, conv_w, conv_b, x_proj_w_t, dt_projs_w_t, dt_projs_b,
          A_logs, Ds, ln_w, ln_b, out_w_t, out):
    def scratch(name, shape):
        return nc.dram_tensor(name, shape, F32, kind="Internal").ap()

    stats0, stats1 = scratch("stats0", (B, 2, S)), scratch("stats1", (B, 2, S))
    x1 = scratch("x1", (B, S, S * S))
    xf = scratch("xf", (S, B, S + 2, S))
    z = scratch("z", (S, B, S * S))
    xc = scratch("xc", (128, NJ, NB, NB, BLK))
    ysum = scratch("ysum", (128, NJ, NB, NB, BLK))
    stats_phase(nc, "s0_", x, stats0, GN_EPS)
    with nc.sbuf_tensor("x1_st", [HALF, GROUPS, STRIPS, 6], F32) as st:
        attention_phase(nc, x.rearrange("c b (s n) -> c (b s) n", s=NW), stats0, Wq, bq, Wk, bk, Wv, bv, Wskip, bskip,
                        x1, st)
        stats_phase(nc, "s1_", None, stats1, GN_EPS, st)
    project_phase(nc, x1, stats1, in_w_t, xf, z)
    conv_phase(nc, xf, conv_w, conv_b, xc)
    scan_phase(nc, xc, ysum, x_proj_w_t, dt_projs_w_t, dt_projs_b, A_logs, Ds)
    final_phase(nc, ysum, z, x1, ln_w, ln_b, out_w_t, out)


def kernel(x, **w):
    import concourse.bacc as bacc
    import numpy as np
    from concourse.bass_utils import run_bass_kernel_spmd

    def plain(name):
        return np.asarray(w[name])

    arrays = {"x": np.asarray(x).transpose(1, 0, 2, 3).reshape(S, B, S * S)}
    for n in ("Wq", "bq", "Wk", "bk", "Wv", "bv", "Wskip", "bskip"):
        arrays[n] = plain("L0_conv_" + n)
    arrays["in_w_t"] = plain("L1_conv_in_proj_w").T
    arrays["conv_w"] = plain("L1_conv_conv_w").reshape(S, 9)
    arrays["conv_b"] = plain("L1_conv_conv_b")
    arrays["x_proj_w_t"] = plain("L1_conv_x_proj_w").transpose(2, 0, 1)
    arrays["dt_projs_w_t"] = plain("L1_conv_dt_projs_w").transpose(2, 0, 1)
    for n in ("dt_projs_b", "A_logs", "Ds", "ln_w", "ln_b"):
        arrays[n] = plain("L1_conv_" + n)
    arrays["out_w_t"] = plain("L1_conv_out_proj_w").T
    arrays = {n: np.ascontiguousarray(a) for n, a in arrays.items()}
    nc = bacc.Bacc("TRN2", target_bir_lowering=False, num_devices=1)
    args = [nc.dram_tensor(n, a.shape, F32, kind="ExternalInput").ap() for n, a in arrays.items()]
    out = nc.dram_tensor("out", (B, S, S * S), F32, kind="ExternalOutput").ap()
    build(nc, *args, out)
    got = run_bass_kernel_spmd(nc, [arrays], core_ids=[0]).results[0]["out"]
    return got.reshape(B, S, S, S)
```
